# Optimizing a Trainium2 kernel written in Bass

```python
import numpy as np
import jax
import jax.numpy as jnp

def _softmax(x, axis=-1):
    return jax.nn.softmax(x, axis=axis)

def _gelu(x):
    return jax.nn.gelu(x, approximate=True)

def _silu(x):
    return jax.nn.silu(x)

def _sigmoid(x):
    return jax.nn.sigmoid(x)

def _layernorm(x, axis=-1, eps=1e-05):
    m = jnp.mean(x, axis=axis, keepdims=True)
    v = jnp.var(x, axis=axis, keepdims=True)
    return (x - m) / jnp.sqrt(v + eps)

def _scatter_add(tgt, idx, src, axis=0):
    return tgt.at[idx].add(src)

def _segment_sum(src, seg, n):
    return jax.ops.segment_sum(src, seg, n)
kernel_name = 'mk_gnn_resnorm_d2_gnn_r8_f751b6'

def setup_inputs(seed: int=0):
    np.random.seed(seed)
    _w = jnp.asarray

    def _rec_inputs():
        import jax
        import jax.numpy as jnp
        _gk = jax.random.key(seed)
        x = -0.000202 + 1 * jax.random.normal(jax.random.fold_in(_gk, 1), (6250, 128), jnp.float32)
        src = jax.random.randint(jax.random.fold_in(_gk, 2), (200000,), 0, 6250, jnp.int32)
        dst = jax.random.randint(jax.random.fold_in(_gk, 3), (200000,), 0, 6250, jnp.int32)
        _o = jnp.argsort(dst, stable=True)
        src = src[_o]
        dst = dst[_o]
        edge_attr_128 = -4.21973e-05 + 0.999841 * jax.random.normal(jax.random.fold_in(_gk, 12), (200000, 128), jnp.float32)
        return (x, src, dst, edge_attr_128)
    x, src, dst, edge_attr_128 = _rec_inputs()

    def _L0_gnn_setup():
        import jax, jax.numpy as jnp
        import numpy as np
        EPS = 1e-05

        def layer_norm(x, g, b):
            m = x.mean(-1, keepdims=True)
            v = ((x - m) ** 2).mean(-1, keepdims=True)
            return (x - m) * jax.lax.rsqrt(v + EPS) * g + b
        H, N, E, F = (8, 6250, 75000, 128)
        D = F // H
        key = jax.random.key(seed)
        ks = jax.random.split(key, 16)
        f32 = jnp.float32
        sF = 1.0 / np.sqrt(F)
        s2D = 1.0 / np.sqrt(2 * D)
        sD = 1.0 / np.sqrt(D)
        inp = {'x_node': jax.random.normal(ks[0], (N, F), f32), 'x_edge': jax.random.normal(ks[1], (E, F), f32), 'src': jax.random.randint(ks[2], (E,), 0, N, jnp.int32), 'dst': jax.random.randint(ks[3], (E,), 0, N, jnp.int32), 'Wq': jax.random.normal(ks[4], (H, F, D), f32) * sF, 'Wk': jax.random.normal(ks[5], (H, F, D), f32) * sF, 'Wv': jax.random.normal(ks[6], (H, F, D), f32) * sF, 'Wke': jax.random.normal(ks[7], (H, F, D), f32) * sF, 'Wve': jax.random.normal(ks[8], (H, F, D), f32) * sF, 'gq': jnp.ones((H, D), f32), 'bq': jnp.zeros((H, D), f32), 'gk': jnp.ones((H, D), f32), 'bk': jnp.zeros((H, D), f32), 'gv': jnp.ones((H, D), f32), 'bv': jnp.zeros((H, D), f32), 'gke': jnp.ones((H, D), f32), 'bke': jnp.zeros((H, D), f32), 'gve': jnp.ones((H, D), f32), 'bve': jnp.zeros((H, D), f32), 'relk_W': jax.random.normal(ks[9], (2 * D, D), f32) * s2D, 'relk_b': jnp.zeros((D,), f32), 'relk_g': jnp.ones((D,), f32), 'relk_beta': jnp.zeros((D,), f32), 'relv_W': jax.random.normal(ks[10], (2 * D, D), f32) * s2D, 'relv_b': jnp.zeros((D,), f32), 'relv_g': jnp.ones((D,), f32), 'relv_beta': jnp.zeros((D,), f32), 'z_W': jax.random.normal(ks[11], (D, D), f32) * sD, 'z_b': jnp.zeros((D,), f32), 'z_g': jnp.ones((D,), f32), 'z_beta': jnp.zeros((D,), f32)}
        return inp
    _L0_gnn_all = _L0_gnn_setup()
    _L0_gnn_in = {k: v for k, v in _L0_gnn_all.items() if k in ('Wq', 'Wk', 'Wv', 'Wke', 'Wve', 'gq', 'bq', 'gk', 'bk', 'gv', 'bv', 'gke', 'bke', 'gve', 'bve', 'relk_W', 'relk_b', 'relk_g', 'relk_beta', 'relv_W', 'relv_b', 'relv_g', 'relv_beta', 'z_W', 'z_b', 'z_g', 'z_beta')}
    del _L0_gnn_all

    def _L1_gnn_setup():
        import jax, jax.numpy as jnp
        import numpy as np
        N = 1250
        E = 80000
        D = 128
        EPS = 1e-08

        def _gcn_conv(x, src, dst, deg_isqrt, W, b, n):
            h = x @ W
            norm = deg_isqrt[src] * deg_isqrt[dst]
            msgs = h[src] * norm[:, None]
            out = jax.ops.segment_sum(msgs, dst, num_segments=n)
            return out + b

        def _pairnorm_pn(x):
            norm = jnp.sqrt(jnp.sum(x * x, axis=1, keepdims=True)) + EPS
            return x / norm
        key = jax.random.key(seed)
        ks = jax.random.split(key, 8)
        x = jax.random.normal(ks[0], (N, D), dtype=jnp.float32)
        edge_index = jax.random.randint(ks[1], (2, E), 0, N, dtype=jnp.int64)
        scale = 1.0 / np.sqrt(D)
        W1 = jax.random.normal(ks[2], (D, D), dtype=jnp.float32) * scale
        b1 = jnp.zeros((D,), dtype=jnp.float32)
        W2 = jax.random.normal(ks[3], (D, D), dtype=jnp.float32) * scale
        b2 = jnp.zeros((D,), dtype=jnp.float32)
        W3 = jax.random.normal(ks[4], (D, D), dtype=jnp.float32) * scale
        b3 = jnp.zeros((D,), dtype=jnp.float32)
        return {'x': x, 'edge_index': edge_index, 'W1': W1, 'b1': b1, 'W2': W2, 'b2': b2, 'W3': W3, 'b3': b3}
    _L1_gnn_all = _L1_gnn_setup()
    _L1_gnn_in = {k: v for k, v in _L1_gnn_all.items() if k in ('W1', 'b1', 'W2', 'b2', 'W3', 'b3')}
    del _L1_gnn_all
    return {'x': x, 'src': src, 'dst': dst, 'edge_attr_128': edge_attr_128, 'L0_gnn_Wq': _L0_gnn_in['Wq'], 'L0_gnn_Wk': _L0_gnn_in['Wk'], 'L0_gnn_Wv': _L0_gnn_in['Wv'], 'L0_gnn_Wke': _L0_gnn_in['Wke'], 'L0_gnn_Wve': _L0_gnn_in['Wve'], 'L0_gnn_gq': _L0_gnn_in['gq'], 'L0_gnn_bq': _L0_gnn_in['bq'], 'L0_gnn_gk': _L0_gnn_in['gk'], 'L0_gnn_bk': _L0_gnn_in['bk'], 'L0_gnn_gv': _L0_gnn_in['gv'], 'L0_gnn_bv': _L0_gnn_in['bv'], 'L0_gnn_gke': _L0_gnn_in['gke'], 'L0_gnn_bke': _L0_gnn_in['bke'], 'L0_gnn_gve': _L0_gnn_in['gve'], 'L0_gnn_bve': _L0_gnn_in['bve'], 'L0_gnn_relk_W': _L0_gnn_in['relk_W'], 'L0_gnn_relk_b': _L0_gnn_in['relk_b'], 'L0_gnn_relk_g': _L0_gnn_in['relk_g'], 'L0_gnn_relk_beta': _L0_gnn_in['relk_beta'], 'L0_gnn_relv_W': _L0_gnn_in['relv_W'], 'L0_gnn_relv_b': _L0_gnn_in['relv_b'], 'L0_gnn_relv_g': _L0_gnn_in['relv_g'], 'L0_gnn_relv_beta': _L0_gnn_in['relv_beta'], 'L0_gnn_z_W': _L0_gnn_in['z_W'], 'L0_gnn_z_b': _L0_gnn_in['z_b'], 'L0_gnn_z_g': _L0_gnn_in['z_g'], 'L0_gnn_z_beta': _L0_gnn_in['z_beta'], 'L1_gnn_W1': _L1_gnn_in['W1'], 'L1_gnn_b1': _L1_gnn_in['b1'], 'L1_gnn_W2': _L1_gnn_in['W2'], 'L1_gnn_b2': _L1_gnn_in['b2'], 'L1_gnn_W3': _L1_gnn_in['W3'], 'L1_gnn_b3': _L1_gnn_in['b3']}

def reference(x, src, dst, edge_attr_128, L0_gnn_Wq, L0_gnn_Wk, L0_gnn_Wv, L0_gnn_Wke, L0_gnn_Wve, L0_gnn_gq, L0_gnn_bq, L0_gnn_gk, L0_gnn_bk, L0_gnn_gv, L0_gnn_bv, L0_gnn_gke, L0_gnn_bke, L0_gnn_gve, L0_gnn_bve, L0_gnn_relk_W, L0_gnn_relk_b, L0_gnn_relk_g, L0_gnn_relk_beta, L0_gnn_relv_W, L0_gnn_relv_b, L0_gnn_relv_g, L0_gnn_relv_beta, L0_gnn_z_W, L0_gnn_z_b, L0_gnn_z_g, L0_gnn_z_beta, L1_gnn_W1, L1_gnn_b1, L1_gnn_W2, L1_gnn_b2, L1_gnn_W3, L1_gnn_b3):
    import jax
    import jax.numpy as jnp

    def _L0_gnn_ref(x_node, x_edge, Wq, Wk, Wv, Wke, Wve, gq, bq, gk, bk, gv, bv, gke, bke, gve, bve, relk_W, relk_b, relk_g, relk_beta, relv_W, relv_b, relv_g, relv_beta, z_W, z_b, z_g, z_beta, src, dst):
        import jax, jax.numpy as jnp
        import numpy as np
        EPS = 1e-05

        def layer_norm(x, g, b):
            m = x.mean(-1, keepdims=True)
            v = ((x - m) ** 2).mean(-1, keepdims=True)
            return (x - m) * jax.lax.rsqrt(v + EPS) * g + b
        N = x_node.shape[0]
        q = layer_norm(jnp.einsum('nf,hfd->hnd', x_node, Wq), gq[:, None, :], bq[:, None, :])
        k = layer_norm(jnp.einsum('nf,hfd->hnd', x_node, Wk), gk[:, None, :], bk[:, None, :])
        v = layer_norm(jnp.einsum('nf,hfd->hnd', x_node, Wv), gv[:, None, :], bv[:, None, :])
        ke = layer_norm(jnp.einsum('ef,hfd->hed', x_edge, Wke), gke[:, None, :], bke[:, None, :])
        ve = layer_norm(jnp.einsum('ef,hfd->hed', x_edge, Wve), gve[:, None, :], bve[:, None, :])
        rel_k = layer_norm(jnp.concatenate([ke, k[:, src]], -1) @ relk_W + relk_b, relk_g, relk_beta)
        qk = jnp.sum(q[:, dst] * rel_k, -1) / 4.0
        qkT = qk.T
        m = jax.ops.segment_max(qkT, dst, num_segments=N)
        se = jax.ops.segment_sum(jnp.exp(qkT - m[dst]), dst, num_segments=N)
        lse = jnp.log(se) + m
        rel_v = layer_norm(jnp.concatenate([ve, v[:, src]], -1) @ relv_W + relv_b, relv_g, relv_beta)
        logw = qk - lse.T[:, dst]
        h = jnp.transpose(logw[..., None] * rel_v, (1, 0, 2))
        agg = jax.ops.segment_sum(h, dst, num_segments=N)
        z = jax.nn.relu(agg @ z_W + z_b)
        z = layer_norm(z, z_g, z_beta)
        return z.reshape(N, -1)

    def _L1_gnn_ref(x, edge_index, W1, b1, W2, b2, W3, b3):
        import jax, jax.numpy as jnp
        import numpy as np
        N = 1250
        E = 80000
        D = 128
        EPS = 1e-08

        def _gcn_conv(x, src, dst, deg_isqrt, W, b, n):
            h = x @ W
            norm = deg_isqrt[src] * deg_isqrt[dst]
            msgs = h[src] * norm[:, None]
            out = jax.ops.segment_sum(msgs, dst, num_segments=n)
            return out + b

        def _pairnorm_pn(x):
            norm = jnp.sqrt(jnp.sum(x * x, axis=1, keepdims=True)) + EPS
            return x / norm
        n = x.shape[0]
        loops = jnp.arange(n, dtype=edge_index.dtype)
        src = jnp.concatenate([edge_index[0], loops])
        dst = jnp.concatenate([edge_index[1], loops])
        deg = jax.ops.segment_sum(jnp.ones_like(dst, dtype=x.dtype), dst, num_segments=n)
        deg_isqrt = jnp.where(deg > 0, jax.lax.rsqrt(jnp.maximum(deg, 1.0)), 0.0)
        prev = x
        for W, b in ((W1, b1), (W2, b2)):
            x = _gcn_conv(x, src, dst, deg_isqrt, W, b, n)
            x = _pairnorm_pn(x)
            x = x + prev
            prev = x
            x = jax.nn.gelu(x, approximate=False)
        return _gcn_conv(x, src, dst, deg_isqrt, W3, b3, n)
    edge_index = jnp.stack([src, dst])
    x = _layernorm(x + _L0_gnn_ref(x, edge_attr_128, L0_gnn_Wq, L0_gnn_Wk, L0_gnn_Wv, L0_gnn_Wke, L0_gnn_Wve, L0_gnn_gq, L0_gnn_bq, L0_gnn_gk, L0_gnn_bk, L0_gnn_gv, L0_gnn_bv, L0_gnn_gke, L0_gnn_bke, L0_gnn_gve, L0_gnn_bve, L0_gnn_relk_W, L0_gnn_relk_b, L0_gnn_relk_g, L0_gnn_relk_beta, L0_gnn_relv_W, L0_gnn_relv_b, L0_gnn_relv_g, L0_gnn_relv_beta, L0_gnn_z_W, L0_gnn_z_b, L0_gnn_z_g, L0_gnn_z_beta, src, dst), axis=-1)
    x = _layernorm(x + _L1_gnn_ref(x, edge_index, L1_gnn_W1, L1_gnn_b1, L1_gnn_W2, L1_gnn_b2, L1_gnn_W3, L1_gnn_b3), axis=-1)
    return x

_drawn_inputs = setup_inputs


def setup_inputs(seed=0):
    import zlib

    import numpy as np

    out = dict(_drawn_inputs(seed))
    spreads = {'L0_gnn_gq': (1.0, 0.6),
     'L0_gnn_bq': (0.0, 0.521),
     'L0_gnn_gk': (1.0, 0.6),
     'L0_gnn_bk': (0.0, 2.0),
     'L0_gnn_gv': (1.0, 0.2),
     'L0_gnn_bv': (0.0, 0.1),
     'L0_gnn_gke': (1.0, 0.542),
     'L0_gnn_bke': (0.0, 2.0),
     'L0_gnn_gve': (1.0, 0.2),
     'L0_gnn_bve': (0.0, 0.1),
     'L0_gnn_relk_b': (0.0, 2.0),
     'L0_gnn_relk_g': (1.0, 0.6),
     'L0_gnn_relk_beta': (0.0, 2.0),
     'L0_gnn_relv_b': (0.0, 0.1),
     'L0_gnn_relv_g': (1.0, 0.2),
     'L0_gnn_relv_beta': (0.0, 0.1),
     'L0_gnn_z_b': (0.0, 0.8),
     'L0_gnn_z_g': (1.0, 0.2),
     'L0_gnn_z_beta': (0.0, 0.1),
     'L1_gnn_b1': (0.0, 2.0),
     'L1_gnn_b2': (0.0, 2.0),
     'L1_gnn_b3': (0.0, 0.1)}
    factors = {'L1_gnn_W1': 3.201, 'L1_gnn_W2': 2.911}
    for name, (base, spread) in spreads.items():
        noise = np.random.default_rng([zlib.crc32(name.encode()), seed]).standard_normal(out[name].shape)
        drawn = base * np.exp(spread * noise) if base else spread * noise
        out[name] = jnp.asarray(drawn.astype(out[name].dtype))
    for name, factor in factors.items():
        out[name] = (out[name] * factor).astype(out[name].dtype)
    return out
```

```python
import concourse.bass as bass
import numpy as np
from concourse import mybir

F32 = mybir.dt.float32
I32 = mybir.dt.int32
ALU = mybir.AluOpType
ACT = mybir.ActivationFunctionType
AX = mybir.AxisListType.X

P = 128
WN = 64
ST = 8
SE = P * ST
NEG = -1.0e30


class Track:

    def __init__(self, sem, lag=None):
        self.sem, self.n, self.ops, self.seen, self.lag = sem, 0, [], {}, lag

    def wait(self, *tokens):
        for sem, val in tokens:
            if self.seen.get(sem.name, 0) < val:
                self.seen[sem.name] = val
                self.ops.append(lambda e, s=sem, v=val: e.wait_ge(s, v))

    def __call__(self, fn, *tokens):
        self.wait(*tokens)
        if self.lag is not None and self.n > self.lag:
            self.wait((self.sem, self.n - self.lag))
        self.n += 1
        self.ops.append(lambda e, s=self.sem: fn(e).then_inc(s, 1))
        return (self.sem, self.n)

    def raw(self, fn, *tokens):
        self.wait(*tokens)
        self.ops.append(fn)

    def now(self):
        return (self.sem, self.n)


class Slot:

    def __init__(self, sem):
        self.sem, self.n = sem, 0

    def dma(self, track, fn, *tokens):
        track.wait(*tokens)
        self.n += 16
        track.ops.append(lambda e: fn(e).then_inc(self.sem, 16))
        return (self.sem, self.n)

    def now(self):
        return (self.sem, self.n)


def gnn(nc, a, out, NW, NS, N):
    from contextlib import ExitStack

    NP = NW * P
    EP = NS * SE
    NC = NP + WN
    NB = EP // 64
    HD = 16

    with ExitStack() as ctx:
        arena = ctx.enter_context(nc.sbuf_tensor("arena", [P, 53100], F32))
        psum = ctx.enter_context(nc.psum_tensor("ps", [P, 8, 512], F32))
        kvp = nc.dram_tensor("kvp", [NP, 256], F32).ap()
        qtab = nc.dram_tensor("qtab", [NP, 136], F32).ap()
        qkd = nc.dram_tensor("qkd", [NB, 512], F32).ap()
        htab = [nc.dram_tensor(f"htab{i}", [NP, P], F32).ap() for i in range(3)]

        sem = lambda n: ctx.enter_context(nc.semaphore(n))
        tracks = {}
        slots = {}
        phase = [0]

        def slot(name):
            name = f"{name}_{phase[0]}"
            if name not in slots:
                slots[name] = Slot(sem("d_" + name))
            return slots[name]

        class Q:
            pass

        q = Q()
        q.V, q.A = Track(sem("s_dve"), 1), Track(sem("s_act"), 1)
        q.E, q.G, q.S = [Track(sem(f"s_{n}")) for n in ("pe", "pool", "sp")]
        allq = [q.V, q.A, q.E, q.G, q.S]

        def join(new=True):
            q.V(lambda e: e.memset(mark[0:1, 8:9], 0.0), q.V.now())
            ends = [t.now() for t in allq if t.n] + [s.now() for s in slots.values() if s.n]
            for t in allq:
                t.wait(*ends)
            if new:
                phase[0] += 1
                for t, n in zip(allq, ("dve", "act", "pe", "pool", "sp")):
                    t.sem, t.n = sem(f"s_{n}{phase[0]}"), 0

        top = [0]

        def mem(*shape, dt=F32, rows=P):
            n = int(np.prod(shape))
            o = top[0]
            top[0] += n
            assert top[0] <= 53100, top[0]
            ap = arena[0:rows, o:o + n]
            if dt is not F32:
                ap = ap.bitcast(dt)
            if len(shape) == 2:
                ap = ap.rearrange("p (a b) -> p a b", b=shape[1])
            if len(shape) == 3:
                ap = ap.rearrange("p (a b c) -> p a b c", b=shape[1], c=shape[2])
            return ap

        def bc(ap, n):
            return ap.unsqueeze(len(ap.shape)).to_broadcast(list(ap.shape) + [n])

        def mid(ap, n):
            return ap.unsqueeze(1).to_broadcast([ap.shape[0], n] + list(ap.shape[1:]))

        def heads(ap):
            return ap.rearrange("p (h d) -> p h d", d=HD)

        def TT(t, o, x, y, op, *w):
            return t(lambda e: e.tensor_tensor(o, x, y, op), *w)

        def TS(t, o, x, s1, s2, op0, op1, *w):
            if s2 is None:
                return t(lambda e: e.tensor_scalar(o, x, s1, None, op0), *w)
            return t(lambda e: e.tensor_scalar(o, x, s1, s2, op0, op1), *w)

        def RED(o, x, op, *w):
            return q.V(lambda e: e.tensor_reduce(o, x, AX, op), *w)

        def RCP(o, x, *w):
            return q.V(lambda e: e.reciprocal(o, x), *w)

        def AC(o, x, f, *w, bias=None, scale=1.0):
            if bias is None:
                return q.A(lambda e: e.activation(o, x, f, scale=scale), *w)
            return q.A(lambda e: e.activation(o, x, f, bias=bias, scale=scale), *w)

        def MM(o, l, r, *w, start=True, stop=True):
            return q.E(lambda e: e.matmul(o, l, r, start=start, stop=stop), *w)

        def TR(o, x, ident, *w):
            return q.E(lambda e: e.transpose(o, x, ident), *w)

        ident = mem(P)
        iota = mem(WN)
        ones = mem(P)
        epsL = mem(1)
        mark = mem(16)
        marks = [0]
        dstrel = mem(NS, ST)
        srci = mem(NS, ST, dt=I32)
        binfo = mem(NS, 2, dt=I32, rows=1)
        deg = mem(NW, 9)
        nbi = mem(1, dt=I32, rows=1)
        perm = top[0]

        s0 = slot("const")
        c_id = s0.dma(q.S, lambda e: e.dma_start(ident, a["ident"]))
        s0.dma(q.S, lambda e: e.dma_start(iota, a["iota"].partition_broadcast(P)))
        c_all = s0.dma(q.S, lambda e: e.dma_start(srci, a["src"].rearrange("p (s t) -> p s t", t=ST)))
        m_one = q.V(lambda e: e.memset(ones, 1.0))
        m_eps = q.V(lambda e: e.memset(epsL, 1e-5))

        dsti = mem(NS * ST, dt=I32)
        dstf = mem(NS, ST)
        bl = mem(2, NS, dt=I32, rows=1)
        blf = mem(2, NS, rows=1)
        nx = mem(NS, dt=I32, rows=1)
        s1 = slot("dst")
        s1.dma(q.S, lambda e: e.dma_start(dsti, a["dst"]))
        s1.dma(q.S, lambda e: e.dma_start(bl[:, 0:1, :].rearrange("p a s -> p (a s)"), a["ends"][0:1, :]))
        d_in = s1.dma(q.S, lambda e: e.dma_start(bl[:, 1:2, :].rearrange("p a s -> p (a s)"), a["ends"][1:2, :]))
        v = q.V(lambda e: e.tensor_copy(dstf, dsti.rearrange("p (s t) -> p s t", t=ST)), d_in)
        v = q.V(lambda e: e.tensor_copy(blf, bl), d_in)
        v1 = q.V(lambda e: e.tensor_copy(binfo[:, :, 0], bl[:, 0, :]), d_in)
        v2 = TT(q.V, blf[:, 1, :], blf[:, 1, :], blf[:, 0, :], ALU.subtract, v)
        v2 = q.V(lambda e: e.tensor_copy(nx, blf[:, 1, :]), v2)
        v_bi = q.V(lambda e: e.tensor_single_scalar(binfo[:, :, 1], nx, 6, ALU.logical_shift_right), v2)
        e1 = MM(psum[:, 0, 0:NS], ones[0:1, :], blf[:, 0, :], v, m_one)
        v_dr = TT(q.V, dstrel, dstf, bc(psum[:, 0, 0:NS], ST), ALU.subtract, e1)

        w5 = mem(5 * 8, HD)
        wm = mem(5 * 8)
        W5 = w5.rearrange("p a d -> p (a d)")
        Wn = W5[:, 0:384]
        W512 = mem(512)
        bdt = mem(2 * 8, HD)
        bdb = mem(2 * 8, HD)
        bm = mem(32)
        cols = mem(8)
        TK = mem(256)
        BK = mem(256)
        wT = mem(256)
        rb = mem(16, HD, rows=1)
        rbm = mem(16, rows=1)
        crow = mem(256, rows=1)
        G1 = mem(P)
        B1 = mem(P)
        G2 = mem(P)
        rows_in = mem(4, P)
        qbc = mem(8)
        s2 = slot("w")
        for i, n in enumerate(("Wq", "Wk", "Wv", "Wke", "Wve")):
            s2.dma(q.S, lambda e, i=i, n=n: e.dma_start(W5[:, i * P:(i + 1) * P], a[n]))
        for i, n in enumerate(("relk", "relv")):
            s2.dma(q.S, lambda e, i=i, n=n: e.dma_start(bdt.rearrange("p a d -> p (a d)")[:, i * P:(i + 1) * P], a[n + "_top"]))
            s2.dma(q.S, lambda e, i=i, n=n: e.dma_start(bdb.rearrange("p a d -> p (a d)")[:, i * P:(i + 1) * P], a[n + "_bot"]))
            s2.dma(q.S, lambda e, i=i, n=n: e.dma_start(rb.rearrange("p a d -> p (a d)")[:, i * P:(i + 1) * P], a[n + "_b"]))
        s2.dma(q.S, lambda e: e.dma_start(cols, a["cols"]))
        for i, n in enumerate(("gq", "bq", "relk_g", "relk_beta")):
            d_w = s2.dma(q.S, lambda e, i=i, n=n: e.dma_start(rows_in[:, i, :], a[n].partition_broadcast(P)))

        def center(x, m, n, *w):
            v = RED(m, x, ALU.add, *w)
            v = TS(q.V, m, m, 1.0 / HD, None, ALU.mult, None, v)
            return TT(q.V, x, x, bc(m, HD), ALU.subtract, v)

        vw = center(w5, wm, 40, d_w)
        vt = center(bdt, bm[:, 0:16], 16, d_w)
        vb = center(bdb, bm[:, 16:32], 16, d_w)
        vr = center(rb, rbm, 16, d_w)
        BT = bdt.rearrange("p a d -> p (a d)")
        BB = bdb.rearrange("p a d -> p (a d)")
        for i in range(2):
            vk = TS(q.V, TK[:, i * P:(i + 1) * P], BT[:, i * P:(i + 1) * P], cols[:, i:i + 1], None, ALU.mult, None, vt)
            vk = TS(q.V, BK[:, i * P:(i + 1) * P], BB[:, i * P:(i + 1) * P], cols[:, 2 + i:3 + i], None, ALU.mult, None, vb)
        t = TR(psum[:, 1, 0:P], W5[:, 384:512], ident, vw, c_all)
        t = TR(psum[:, 1, P:2 * P], W5[:, 512:640], ident)
        v = q.V(lambda e: e.tensor_copy(wT, psum[:, 1, 0:256]), t)
        v = q.V(lambda e: e.tensor_copy(W512[:, 0:256], W5[:, 384:640]))
        for i in range(2):
            t = MM(psum[:, 2, i * P:(i + 1) * P], wT[:, i * P:(i + 1) * P], TK[:, i * P:(i + 1) * P], v)
        v_w5 = q.V(lambda e: e.tensor_copy(W512[:, 256:512], psum[:, 2, 0:256]), t)
        for i in range(2):
            o = psum[0:1, 3, i * P:(i + 1) * P]
            MM(o, cols[:, 4 + i:5 + i], BT[:, i * P:(i + 1) * P], stop=False)
            MM(o, cols[:, 6 + i:7 + i], BB[:, i * P:(i + 1) * P], start=False, stop=False)
            t = MM(o, ones[0:1, 0:1], rb.rearrange("p a d -> p (a d)")[:, i * P:(i + 1) * P], vr, start=False)
        v_c = q.V(lambda e: e.tensor_copy(crow, psum[0:1, 3, 0:256]), t)
        v = TS(q.V, rows_in[:, 2:4, :], rows_in[:, 2:4, :], 0.25, None, ALU.mult, None, d_w)
        TT(q.V, G1, rows_in[:, 0, :], rows_in[:, 2, :], ALU.mult, v)
        TT(q.V, B1, rows_in[:, 1, :], rows_in[:, 2, :], ALU.mult)
        TT(q.V, G2, rows_in[:, 0, :], rows_in[:, 3, :], ALU.mult)
        v = TT(q.V, rows_in[:, 1, :], rows_in[:, 1, :], rows_in[:, 3, :], ALU.mult, q.V.now())
        v_g = RED(qbc, heads(rows_in[:, 1, :]), ALU.add, v)

        nsq = mem(2, 384)
        nva = mem(2, 24)
        nsd = mem(2, 24)
        nh = mem(2, 384)
        nq = mem(2, 136)
        nqt = mem(2, P)
        nT = mem(2, 256)
        nkv = mem(2, 256)
        xt = mem(2, P)
        hist = {}

        def nA(w):
            b = w % 2
            d = slot(f"xt{b}").dma(q.S, lambda e: e.dma_start(xt[:, b, :], a["xT"][:, w * P:(w + 1) * P]),
                                   *([hist["mm", w - 2]] if w > 1 else []))
            t = MM(psum[:, b, 0:384], xt[:, b, :], Wn, d, v_w5, *([hist["h", w - 2]] if w > 1 else []))
            hist["mm", w] = t
            s = AC(nsq[:, b, :], psum[:, b, 0:384], ACT.Square, t, *([hist["var", w - 2]] if w > 1 else []))
            r = RED(nva[:, b, :], heads(nsq[:, b, :]), ALU.add, s)
            hist["var", w] = r
            hist["sd", w] = AC(nsd[:, b, :], nva[:, b, :], ACT.Sqrt, r, m_eps, bias=epsL, scale=1.0 / HD)

        def nB(w):
            b = w % 2
            r = RCP(nva[:, b, :], nsd[:, b, :], hist["sd", w])
            pre = [hist["tr", w - 2]] if w > 1 else []
            h = TT(q.V, heads(nh[:, b, :]), heads(psum[:, b, 0:384]), bc(nva[:, b, :], HD), ALU.mult, r, *pre)
            hist["h", w] = h
            TR(psum[:, 2 + b, 0:P], nh[:, b, P:2 * P], ident, h, *([hist["cT", w - 2]] if w > 1 else []))
            t = TR(psum[:, 2 + b, P:256], nh[:, b, 256:384], ident)
            hist["tr", w] = t
            hist["cT", w] = AC(nT[:, b, :], psum[:, 2 + b, 0:256], ACT.Copy, t,
                               *([hist["mm2", w - 2]] if w > 1 else []))
            pre = [slot(f"qo{b}").now()] if w > 1 else []
            m = TT(q.V, nqt[:, b, :], nh[:, b, 0:P], G2, ALU.mult, v_g, h)
            m1 = TT(q.V, nq[:, b, 0:P], nh[:, b, 0:P], G1, ALU.mult, *pre)
            r = RED(nq[:, b, P:136], heads(nqt[:, b, :]), ALU.add, m)
            TT(q.V, nq[:, b, 0:P], nq[:, b, 0:P], B1, ALU.add, m1)
            t = TT(q.V, nq[:, b, P:136], nq[:, b, P:136], qbc, ALU.add, r)
            slot(f"qo{b}").dma(q.S, lambda e: e.dma_start(qtab[w * P:(w + 1) * P, :], nq[:, b, :]), t)

        def nC(w):
            b = w % 2
            for i in range(2):
                o = psum[:, 4 + b, i * P:(i + 1) * P]
                MM(o, nT[:, b, i * P:(i + 1) * P], BK[:, i * P:(i + 1) * P], hist["cT", w],
                   *([hist["kv", w - 2]] if w > 1 else []), stop=False)
                t = MM(o, ones[0:1, :], crow[:, i * P:(i + 1) * P], v_c, start=False)
            hist["mm2", w] = t
            c = AC(nkv[:, b, :], psum[:, 4 + b, 0:256], ACT.Copy, t,
                   *([slot(f"ko{b}").now()] if w > 1 else []))
            hist["kv", w] = c
            slot(f"ko{b}").dma(q.S, lambda e: e.dma_start(kvp[w * P:(w + 1) * P, :], nkv[:, b, :]), c)

        for w in range(NW + 2):
            if w < NW:
                nA(w)
            if 0 < w <= NW:
                nB(w - 1)
            if w > 1:
                nC(w - 2)

        join()

        W512b = W512
        save = top[0]
        top[0] = perm
        W = mem(512)
        v_w = q.V(lambda e: e.tensor_copy(W, W512b))
        acc = mem(2, NC)
        accq = mem(NC, rows=9)
        XB = 3
        xe = mem(XB, SE)
        GB = 3
        kg = mem(GB, ST, 256)
        qg = mem(GB, ST, 136)
        tu = mem(2, ST, 256)
        sq = mem(2, 512)
        va = mem(3, 32)
        sd = mem(3, 32)
        sq2 = mem(ST, 256)
        va2 = mem(ST, HD)
        sd2 = mem(ST, HD)
        pr = mem(ST, P)
        qr = mem(ST, 8)
        qs = mem(2, ST, 8)
        c1 = mem(ST, 8)
        vals = mem(2, ST * 265)
        agS = mem(265, rows=WN)
        oh = mem(2, ST, WN)
        dc = mem(ST)
        q.V.wait(v_w)
        V0 = q.V(lambda e: e.memset(acc, 0.0), v_w)
        V1 = q.V(lambda e: e.memset(accq, 0.0))
        V2 = q.V(lambda e: e.memset(vals, 1.0))
        xcnt = {}

        def val(b):
            return vals[:, b, :].rearrange("p (t f) -> p t f", f=265)

        regs = {}
        sx = {n: sem("x_" + n) for n in ("dve", "pe", "in", "act", "pt")}

        def init_regs(e, name):
            regs[name] = e.alloc_register("xc_" + name)
            e.reg_mov(regs[name], 0)

        q.V.raw(lambda e: init_regs(e, "dve"))
        q.V.raw(lambda e: init_regs(e, "at"))
        q.V.raw(lambda e: init_regs(e, "in"))
        q.E.raw(lambda e: init_regs(e, "pe"), v_bi)
        q.A.raw(lambda e: init_regs(e, "act"), v_bi)

        def pe_aggregate(s, parts, o_h, *w):
            b = s % 2
            for dst, lhs in parts[:-1]:
                for t in range(ST):
                    q.E.raw(lambda e, dst=dst, lhs=lhs, t=t: e.matmul(dst, lhs(t), o_h[:, t, :], start=t == 0, stop=t == ST - 1), *w)
            dst, lhs = parts[-1]
            for t in range(ST - 1):
                q.E.raw(lambda e, t=t: e.matmul(dst, lhs(t), o_h[:, t, :], start=t == 0, stop=False), *w)
            return q.E(lambda e: e.matmul(dst, lhs(ST - 1), o_h[:, ST - 1, :], start=False, stop=True))

        def pe_more(s, parts, o_h, sx):
            def f(e):
                n = e.value_load(binfo[0:1, s, 1:2], min_val=0, max_val=NP // WN)
                with e.If(n > 0), e.Fori(0, n) as i:
                    e.reg_add(regs["pe"], regs["pe"], 1)
                    e.wait_ge(sx["dve"], e.snap(regs["pe"], min_val=1, max_val=1 << 20))
                    last = None
                    for dst, lhs in parts:
                        for t in range(ST):
                            last = e.matmul(dst, lhs(t), o_h[:, t, :], start=t == 0, stop=t == ST - 1)
                    last.then_inc(sx["pe"], 1)
            q.E.raw(f)

        def dve_add(s, adds, o_h, dc, sx, *w):
            q.V.wait(*w)
            q.V.n += len(adds) + 2
            q_sem, done, na = q.V.sem, q.V.n - 1, len(adds)
            marks[0] = (marks[0] + 1) % 8
            m = marks[0]

            def f(e):
                n0 = e.value_load(binfo[0:1, s, 0:1], min_val=0, max_val=NP)
                for tgt, src in adds:
                    o = tgt(n0)
                    e.tensor_tensor(o, o, src, ALU.add).then_inc(q_sem, 1)
                e.tensor_copy(dc, dstrel[:, s, :]).then_inc(q_sem, 1)
                n = e.value_load(binfo[0:1, s, 1:2], min_val=0, max_val=NP // WN)
                e.reg_mov(regs["at"], n0)
                with e.If(n > 0), e.Fori(0, n) as i:
                    e.reg_add(regs["at"], regs["at"], WN)
                    at = e.snap(regs["at"], min_val=0, max_val=NP)
                    k = e.snap(regs["dve"], min_val=0, max_val=1 << 20)
                    ki = e.snap(regs["in"], min_val=0, max_val=1 << 20)
                    e.wait_ge(q_sem, done)
                    e.tensor_scalar(dc, dc, float(-WN), None, ALU.add).then_inc(sx["in"], 1)
                    e.wait_ge(sx["in"], ki + 1)
                    e.tensor_tensor(o_h, bc(dc, WN), mid(iota, ST), ALU.is_equal).then_inc(sx["dve"], 1)
                    e.wait_ge(sx["pe"], k + 1)
                    for tgt, src in adds:
                        o = tgt(at)
                        e.tensor_tensor(o, o, src, ALU.add).then_inc(sx["in"], 1)
                    e.wait_ge(sx["in"], ki + (1 + na))
                    e.reg_add(regs["dve"], regs["dve"], 1)
                    e.reg_add(regs["in"], regs["in"], 1 + na)
                e.memset(mark[0:1, m:m + 1], 0.0).then_inc(q_sem, 1)
            q.V.ops.append(f)
            return (q_sem, done + 1)

        H = {}

        def get(*k):
            return [H[k]] if k in H else []

        GR = ST // 2

        def load(s):
            b = s % XB
            d = slot(f"xe{b}").dma(q.S, lambda e: e.dma_start(xe[:, b, :], a["xe"][s]), *get("mm", s - XB, GR - 1))
            H["x", s] = d

        def gather(s):
            b = s % GB
            q.G.wait(*get("u", s - GB))
            for t in range(ST):
                ix = srci[:, s, t:t + 1]
                H["kg", s] = slot(f"kg{b}").dma(q.G, lambda e, t=t, ix=ix: e.indirect_dma_start(
                    kg[:, b, t, :], None, kvp, bass.IndirectOffsetOnAxis(ap=ix, axis=0)))
            q.G.wait(*get("qb", s - GB))
            for t in range(ST):
                ix = dsts[:, s, t:t + 1]
                H["qg", s] = slot(f"qg{b}").dma(q.G, lambda e, t=t, ix=ix: e.indirect_dma_start(
                    qg[:, b, t, :], None, qtab, bass.IndirectOffsetOnAxis(ap=ix, axis=0)))

        dsts = mem(NS, ST, dt=I32)
        d_ds = slot("dsts").dma(q.S, lambda e: e.dma_start(dsts, a["dst"].rearrange("p (s t) -> p s t", t=ST)))
        q.G.wait(d_ds)

        def grp(s, g):
            k = s * GR + g
            ps = psum[:, 2 * (k % 3):2 * (k % 3) + 2, :]
            for j in range(2):
                t = 2 * g + j
                H["mm", s, g] = MM(ps[:, j, :], xe[:, s % XB, t * P:(t + 1) * P], W, H["x", s], v_w,
                                   *get("tm", k - 3))
            b = k % 2
            H["sq", k] = AC(sq[:, b, :].rearrange("p (j f) -> p j f", j=2), ps[:, :, 0:256], ACT.Square, H["mm", s, g],
                            *get("va", k - 2))

        def grp1(k):
            H["va", k] = RED(va[:, k % 3, :], heads(sq[:, k % 2, :]), ALU.add, H["sq", k], *get("tm", k - 3))

        def grp2(k):
            b = k % 3
            H["sd", k] = AC(sd[:, b, :], va[:, b, :], ACT.Sqrt, H["va", k], *get("tm", k - 3), bias=epsL, scale=1.0 / HD)

        def grp3(k):
            s, g, b = k // GR, k % GR, k % 3
            ps = psum[:, 2 * (k % 3):2 * (k % 3) + 2, 256:512]
            r = RCP(va[:, b, :], sd[:, b, :], H["sd", k])
            o = tu[:, s % 2, 2 * g:2 * g + 2, :].rearrange("p j (h d) -> p j h d", d=HD)
            H["tm", k] = TT(q.V, o, ps.rearrange("p j (h d) -> p j h d", d=HD),
                            bc(va[:, b, :].rearrange("p (j h) -> p j h", j=2), HD), ALU.mult, r,
                            *get("sq2", s - 2))

        def sup1(s):
            b = s % 2
            u = tu[:, b, :, :]
            H["u", s] = TT(q.V, u, u, kg[:, s % GB, :, :], ALU.add, H["kg", s], H["tm", s * GR + GR - 1])
            H["sq2", s] = AC(sq2, u, ACT.Square, H["u", s], *get("va2", s - 1))
            H["pr", s] = TT(q.V, pr, u[:, :, 0:P], qg[:, s % GB, :, 0:P], ALU.mult, H["u", s], H["qg", s])
            H["qb", s] = q.V(lambda e: e.tensor_copy(c1, qg[:, s % GB, :, P:136]))

        def sup2(s):
            H["qr", s] = RED(qr, pr.rearrange("p t (h d) -> p t h d", d=HD), ALU.add, H["pr", s])
            H["va2", s] = RED(va2, sq2.rearrange("p t (h d) -> p t h d", d=HD), ALU.add, H["sq2", s], *get("sd2", s - 1))
            H["sd2", s] = AC(sd2, va2, ACT.Sqrt, H["va2", s], *get("r2", s - 1), bias=epsL, scale=1.0 / HD)

        def sup3(s):
            b = s % 2
            u = tu[:, b, :, :].rearrange("p t (h d) -> p t h d", d=HD)
            r = RCP(va2, sd2, H["sd2", s])
            H["r2", s] = r
            m = TT(q.V, qs[:, b, :, :], qr, va2[:, :, 0:8], ALU.mult, r, H["qr", s], *get("qo", s - 2), *get("q9", s - 2))
            m = TT(q.V, qs[:, b, :, :], qs[:, b, :, :], c1, ALU.add, m, H["qb", s])
            H["qo", s] = slot(f"qo{b}").dma(q.S, lambda e: e.dma_start(
                qkd[s * 16:(s + 1) * 16, :].rearrange("a (p f) -> (a p) f", f=64), qs[:, b, :, :]), m)
            H["q9", s] = AC(val(b)[:, :, 257:265], qs[:, b, :, :], ACT.Copy, m, V2, *get("add", s - 2))
            H["m2", s] = TT(q.V, c1, qs[:, b, :, :], va2[:, :, 8:16], ALU.mult, m)

        def sup4(s):
            b = s % 2
            u = tu[:, b, :, :].rearrange("p t (h d) -> p t h d", d=HD)
            BV = val(b)[:, :, P:256].rearrange("p t (h d) -> p t h d", d=HD)
            AV = val(b)[:, :, 0:P].rearrange("p t (h d) -> p t h d", d=HD)
            TT(q.V, BV, u[:, :, 8:16, :], bc(va2[:, :, 8:16], HD), ALU.mult, *get("ag", s - 2))
            TT(q.V, AV, u[:, :, 8:16, :], bc(c1, HD), ALU.mult, H["m2", s])
            H["oh", s] = TT(q.V, oh[:, b, :, :], bc(dstrel[:, s, :], WN), mid(iota, ST), ALU.is_equal)

        def agg_tile(e, s, t, o_h):
            return e.matmul(psum[0:WN, 6, 0:265], o_h[:, t, :], val(s % 2)[:, t, :], start=t == 0, stop=t == ST - 1)

        def turned(e, k):
            if k < 2:
                return e.transpose(psum[:, 7, k * WN:(k + 1) * WN], agS[:, k * P:(k + 1) * P], ident[0:WN, 0:WN])
            return e.transpose(psum[0:9, 7, 2 * WN:3 * WN], agS[:, 256:265], ident[0:WN, 0:WN])

        def agg(s, tiles):
            for t in tiles:
                H["ag", s] = q.E(lambda e, t=t: agg_tile(e, s, t, oh[:, s % 2, :, :]), H["oh", s], H["q9", s],
                                 *get("ev", s - 1))

        def evac(s):
            H["ev", s] = AC(agS, psum[0:WN, 6, 0:265], ACT.Copy, H["ag", s], *get("tr", s - 1))

        def tail(s):
            for k in range(3):
                H["tr", s] = q.E(lambda e, k=k: turned(e, k), H["ev", s], *get("add", s - 1))

            def pe_extra(e):
                n = e.value_load(binfo[0:1, s, 1:2], min_val=0, max_val=NP // WN)
                with e.If(n > 0), e.Fori(0, n) as i:
                    k = e.snap(regs["pe"], min_val=0, max_val=1 << 20)
                    e.wait_ge(sx["dve"], k + 1)
                    for t in range(ST):
                        last = agg_tile(e, s, t, oh[:, s % 2, :, :])
                    last.then_inc(sx["pe"], 1)
                    e.wait_ge(sx["act"], k + 1)
                    e.reg_add(regs["pe"], regs["pe"], 1)
                    for j in range(3):
                        last = turned(e, j)
                    last.then_inc(sx["pt"], 1)

            def act_extra(e):
                n = e.value_load(binfo[0:1, s, 1:2], min_val=0, max_val=NP // WN)
                with e.If(n > 0), e.Fori(0, n) as i:
                    k = e.snap(regs["act"], min_val=0, max_val=1 << 20)
                    e.wait_ge(sx["pe"], k + 1)
                    e.activation(agS, psum[0:WN, 6, 0:265], ACT.Copy).then_inc(sx["act"], 1)
                    e.reg_add(regs["act"], regs["act"], 1)

            q.E.raw(pe_extra)
            q.A.raw(act_extra, H["tr", s])
            bank = psum[:, 7, :]
            H["add", s] = dve_add(s, [
                (lambda n: acc[:, :, bass.ds(n, WN)], bank[:, 0:2 * WN].rearrange("p (x n) -> p x n", n=WN)),
                (lambda n: accq[:, bass.ds(n, WN)], bank[0:9, 2 * WN:3 * WN]),
            ], oh[:, s % 2, :, :], dc, {**sx, "pe": sx["pt"]}, H["tr", s], *get("add", s - 1), V1)

        for s in range(2):
            load(s)
            gather(s)
        grp(0, 0)
        for s in range(NS + 1):
            for g in range(GR):
                k = s * GR + g
                if s < NS and g == 1 and s + 2 < NS:
                    load(s + 2)
                if k + 1 < NS * GR:
                    grp((k + 1) // GR, (k + 1) % GR)
                if 0 <= k - 1 < NS * GR:
                    grp3(k - 1)
                if s < NS:
                    grp1(k)
                    grp2(k)
                if s >= 1:
                    if g == 1:
                        sup1(s - 1)
                        if s + 1 < NS:
                            gather(s + 1)
                    if g == 2:
                        sup2(s - 1)
                    if g == 3:
                        sup3(s - 1)
                if s >= 2:
                    if g == 0:
                        sup4(s - 2)
                    if g == 1:
                        agg(s - 2, range(0, 4))
                    if g == 2:
                        agg(s - 2, range(4, 8))
                        evac(s - 2)
                    if g == 3:
                        tail(s - 2)
        sup4(NS - 1)
        agg(NS - 1, range(0, 8))
        evac(NS - 1)
        tail(NS - 1)
        join()

        top[0] = perm
        W = mem(512)
        acc = mem(2, NC)
        accq = mem(NC, rows=9)
        lse = mem(NW, 8)
        ends = mem(NW)
        begs = mem(NW)
        phase3 = max(top[0], perm + 6 * P + NW * P + 2 * ST * (P + WN) + ST + 2 * P + NC)
        top[0] = phase3
        cs = mem(NP, rows=1)
        zer = mem(NP, rows=1)
        bi = mem(NW, dt=I32)
        bf = mem(NW)
        nbk = mem(NW)
        nbt = mem(P, rows=1)
        nbm = mem(1, rows=1)
        m0 = q.V(lambda e: e.memset(zer, 0.0))
        v = q.V(lambda e: e.tensor_tensor_scan(cs, accq[0:1, 0:NP], zer, 0.0, ALU.add, ALU.add), m0)
        for w in range(NW):
            t1 = MM(psum[:, w // 32, (w % 32) * 9:(w % 32) * 9 + 9], accq[:, w * P:(w + 1) * P], ident[0:9, 0:9])
        for w in range(NW):
            t2 = MM(psum[:, 2, w:w + 1], cs[0:1, w * P:(w + 1) * P], ones[0:1, 0:1], v)
        nw0 = min(NW, 32)
        q.V(lambda e: e.tensor_copy(deg[:, 0:nw0, :], psum[:, 0, 0:nw0 * 9].rearrange("p (w c) -> p w c", c=9)), t1)
        if NW > 32:
            q.V(lambda e: e.tensor_copy(deg[:, 32:NW, :], psum[:, 1, 0:(NW - 32) * 9].rearrange("p (w c) -> p w c", c=9)))
        v = q.V(lambda e: e.tensor_copy(ends, psum[:, 2, 0:NW]), t2)
        v = TT(q.V, begs, ends, deg[:, :, 0], ALU.subtract, v)
        v = q.V(lambda e: e.tensor_copy(bi, begs), v)
        v = q.V(lambda e: e.tensor_single_scalar(bi, bi, 6, ALU.logical_shift_right), v)
        v = q.V(lambda e: e.tensor_copy(bf, bi), v)
        b64 = mem(NW)
        v1 = TS(q.V, b64, bf, 64.0, None, ALU.mult, None, v)
        v = TT(q.V, begs, begs, b64, ALU.subtract, v1)
        v = TT(q.V, ends, ends, b64, ALU.subtract, v)
        v = RED(nbk[:, 0:1], ends, ALU.max, v)
        t = TR(psum[0:1, 3, 0:P], nbk[:, 0:1], ident, v)
        v = q.V(lambda e: e.tensor_reduce(nbm, psum[0:1, 3, 0:P], AX, ALU.max), t)
        v = TS(q.V, nbm, nbm, 63.0 - 128.0, 0.0, ALU.add, ALU.max, v)
        v = q.V(lambda e: e.tensor_copy(nbi, nbm), v)
        v_nb = q.V(lambda e: e.tensor_single_scalar(nbi, nbi, 6, ALU.logical_shift_right), v)
        join()

        GW = 7
        ck = mem(GW, 128 * 8)
        mk = mem(GW, 128)
        mk2 = mem(GW, 128)
        bidx = mem(GW * 2, dt=I32)
        bjf = mem(GW)
        mx = mem(GW, 8)
        mn = mem(GW, 8)
        cr = mem(GW, 8)
        se = mem(GW, 8)
        sj = mem(GW, 8)
        jo = mem(2)
        iot2 = mem(2 * WN)
        ss = mem(NW, 8)
        mm_ = mem(NW, 8)
        q.V(lambda e: e.tensor_copy(iot2[:, 0:WN], iota))
        v_i2 = TS(q.V, iot2[:, WN:], iota, float(WN), None, ALU.add, None)
        s_lv, s_la, s_lg = sem("l_dve"), sem("l_act"), sem("l_pool")
        q.V.raw(lambda e: init_regs(e, "lv"))
        q.V.raw(lambda e: init_regs(e, "li"))
        q.A.raw(lambda e: init_regs(e, "la"))
        q.G.raw(lambda e: init_regs(e, "lg"))

        def masked(T, x, b0, b1, it, n, w0, gw, prev):
            m = mk[:, 0:gw, 0:n]
            m2 = mk2[:, 0:gw, 0:n]
            i_ = it.unsqueeze(1).to_broadcast([P, gw, n])
            v = T(lambda e: e.tensor_tensor(m, i_, bc(b0, n), ALU.is_ge), prev)
            v = T(lambda e: e.tensor_tensor(m2, i_, bc(b1, n), ALU.is_lt), v)
            v = T(lambda e: e.tensor_tensor(m, m, m2, ALU.mult), v)
            v = T(lambda e: e.tensor_scalar(m, m, -NEG, NEG, ALU.mult, ALU.add), v)
            x3 = x
            v = T(lambda e: e.tensor_tensor(x3, x3, bc(m, 8), ALU.add), v)
            return v

        rounds = {n: sem("l_" + n) for n in ("jo", "j2", "jo2")}

        def log_sum(w0):
            gw = min(GW, NW - w0)
            b0, b1 = begs[:, w0:w0 + gw], ends[:, w0:w0 + gw]
            bfw = bf[:, w0:w0 + gw]
            v = None
            for j in range(2):
                v = TS(q.V, bjf[:, 0:gw], bfw, float(j), float(NB - 1), ALU.add, ALU.min, v_i2, q.V.now())
                v = q.V(lambda e, j=j: e.tensor_copy(bidx[:, j * GW:j * GW + gw], bjf[:, 0:gw]), v)
            for i in range(gw):
                for j in range(2):
                    dk = slot("ck").dma(q.G, lambda e, i=i, j=j: e.indirect_dma_start(
                        ck[:, i, j * 512:(j + 1) * 512], None, qkd,
                        bass.IndirectOffsetOnAxis(ap=bidx[:, j * GW + i:j * GW + i + 1], axis=0)), v)
            X = ck[:, 0:gw, :].rearrange("p w (i h) -> p w i h", h=8)
            v = masked(q.V, X, b0, b1, iot2, 128, w0, gw, dk)
            XH = ck[:, 0:gw, :].rearrange("p w (i h) -> p w h i", h=8)
            m_, s_ = mx[:, 0:gw, :], se[:, 0:gw, :]
            v = RED(m_, XH, ALU.max, v)
            v = TT(q.V, X, X, m_.unsqueeze(2).to_broadcast([P, gw, 128, 8]), ALU.subtract, v)
            t = AC(ck[:, 0:gw, :], ck[:, 0:gw, :], ACT.Exp, v)
            v = RED(s_, XH, ALU.add, t)

            s_ld = sem(f"l_dma{w0}")
            s_jo, s_j2, s_jo2 = rounds["jo"], rounds["j2"], rounds["jo2"]
            sem_v, done = q.V.sem, q.V.n

            def pool_more(e, s_ld=s_ld, gw=gw):
                n = e.value_load(nbi[0:1, 0:1], min_val=0, max_val=NB)
                with e.If(n > 0), e.Fori(0, n) as j:
                    k = e.snap(regs["lg"], min_val=0, max_val=1 << 16)
                    e.wait_ge(s_lg, k + 1)
                    e.reg_add(regs["lg"], regs["lg"], 1)
                    for i in range(gw):
                        e.indirect_dma_start(ck[:, i, 0:512], None, qkd,
                                             bass.IndirectOffsetOnAxis(ap=bidx[:, i:i + 1], axis=0)).then_inc(s_ld, 16)

            def act_more(e, w0=w0, gw=gw):
                n = e.value_load(nbi[0:1, 0:1], min_val=0, max_val=NB)
                with e.If(n > 0), e.Fori(0, n) as j:
                    ki = e.snap(regs["la"], min_val=0, max_val=1 << 20)
                    e.wait_ge(s_lv, ki + (NSTEP - NTAIL))
                    e.reg_add(regs["la"], regs["la"], NSTEP)
                    e.activation(cr[:, 0:gw, :], cr[:, 0:gw, :], ACT.Exp).then_inc(s_la, 1)
                    e.activation(ck[:, 0:gw, 0:512], ck[:, 0:gw, 0:512], ACT.Exp).then_inc(s_la, 1)

            NSTEP, NTAIL = 17, 4

            def dve_more(e, s_ld=s_ld, sem_v=sem_v, done=done, w0=w0, gw=gw, b0=b0, b1=b1, bfw=bfw, m_=m_, s_=s_):
                n = e.value_load(nbi[0:1, 0:1], min_val=0, max_val=NB)
                X = ck[:, 0:gw, 0:512].rearrange("p w (i h) -> p w i h", h=8)
                XH = ck[:, 0:gw, 0:512].rearrange("p w (i h) -> p w h i", h=8)
                n_, c_, j_ = mn[:, 0:gw, :], cr[:, 0:gw, :], sj[:, 0:gw, :]
                step = [0]
                e.wait_ge(sem_v, done)
                e.memset(jo, 2.0).then_inc(s_jo, 1)
                e.wait_ge(s_jo, w0 // GW + 1)
                with e.If(n > 0), e.Fori(0, n) as j:
                    k = e.snap(regs["lv"], min_val=0, max_val=1 << 16)
                    ki = e.snap(regs["li"], min_val=0, max_val=1 << 20)

                    def do(ins):
                        step[0] += 1
                        ins.then_inc(s_lv, 1)
                        e.wait_ge(s_lv, ki + step[0])
                    T = lambda fn, *w: do(fn(e))
                    do(e.tensor_tensor(bjf[:, 0:gw], bfw, jo[:, 0:1].to_broadcast([P, gw]), ALU.add))
                    do(e.tensor_scalar(bidx[:, 0:gw], bjf[:, 0:gw], float(NB - 1), None, ALU.min))
                    e.sem_inc(s_lg, 1)
                    do(e.tensor_scalar(jo[:, 1:2], jo[:, 0:1], 64.0, None, ALU.mult))
                    do(e.tensor_tensor(iot2[:, WN:], iota, jo[:, 1:2].to_broadcast([P, WN]), ALU.add))
                    e.wait_ge(s_ld, (j + 1) * (16 * gw))
                    masked(T, X, b0, b1, iot2[:, WN:], WN, w0, gw, None)
                    do(e.tensor_reduce(n_, XH, AX, ALU.max))
                    do(e.tensor_tensor(n_, n_, m_, ALU.max))
                    do(e.tensor_tensor(c_, m_, n_, ALU.subtract))
                    do(e.tensor_tensor(X, X, n_.unsqueeze(2).to_broadcast([P, gw, WN, 8]), ALU.subtract))
                    assert step[0] == NSTEP - NTAIL, step
                    e.wait_ge(s_la, k * 2 + 2)
                    do(e.tensor_tensor(s_, s_, c_, ALU.mult))
                    do(e.tensor_reduce(j_, XH, AX, ALU.add))
                    do(e.tensor_tensor(s_, s_, j_, ALU.add))
                    e.tensor_copy(m_, n_).then_inc(s_lv, 1)
                    e.wait_ge(s_lv, ki + NSTEP)
                    e.tensor_scalar(jo[:, 0:1], jo[:, 0:1], 1.0, None, ALU.add).then_inc(s_j2, 1)
                    e.wait_ge(s_j2, k + 1)
                    e.reg_add(regs["lv"], regs["lv"], 1)
                    e.reg_add(regs["li"], regs["li"], NSTEP)
                e.tensor_scalar(iot2[:, WN:], iota, float(WN), None, ALU.add).then_inc(s_jo2, 1)
                e.wait_ge(s_jo2, w0 // GW + 1)
            q.G.raw(pool_more)
            q.A.raw(act_more)
            q.V.raw(dve_more)
            q.V(lambda e, w0=w0, gw=gw, s_=s_: e.tensor_copy(ss[:, w0:w0 + gw, :], s_))
            return q.V(lambda e, w0=w0, gw=gw, m_=m_: e.tensor_copy(mm_[:, w0:w0 + gw, :], m_))

        for w0 in range(0, NW, GW):
            v = log_sum(w0)
        t = AC(ss, ss, ACT.Ln, v)
        v = TT(q.V, lse, ss, mm_, ALU.add, t)
        join()

        top[0] = phase3
        x1 = mem(NW, P)
        x1s = top[0]
        dis = mem(NW)
        zg_in = mem(3, P)
        zw = mem(P)
        zgw = mem(P)
        c2 = mem(2)
        bz = mem(P)
        bzr = mem(P, rows=1)
        s3 = slot("z")
        for i, n in enumerate(("z_b", "z_g", "z_beta")):
            s3.dma(q.S, lambda e, i=i, n=n: e.dma_start(zg_in[:, i, :], a[n].partition_broadcast(P)))
        s3.dma(q.S, lambda e: e.dma_start(zw, a["zw"]))
        d3 = s3.dma(q.S, lambda e: e.dma_start(c2, a["relv_cols"]))
        v_z = TS(q.V, zgw, zw, c2[:, 0:1], None, ALU.mult, None, d3)
        t = MM(psum[0:1, 7, 0:P], c2[:, 1:2], zw, d3)
        v = q.V(lambda e: e.tensor_copy(bzr, psum[0:1, 7, 0:P]), t)
        t = MM(psum[:, 7, P:2 * P], ones[0:1, :], bzr, v)
        v_bz = q.V(lambda e: e.tensor_copy(bz, psum[:, 7, P:2 * P]), t)
        v = TS(q.V, dis, deg[:, :, 0], 1.0, None, ALU.add, None)
        t = AC(dis, dis, ACT.Sqrt, v)
        v_dis = RCP(dis, dis, t)
        g4 = 4
        z = mem(2, g4 * P)
        zt = mem(2, g4 * P)
        xn = mem(2, g4 * P)
        hm = mem(2, g4 * 8)
        hs = mem(2, g4 * 8)
        nm = mem(2, g4)
        Hn = {}

        def layer_norm_nodes(x, tmp, m, s, n, d, g, *w):
            v = RED(m, x, ALU.add, *w)
            v = TS(q.V, m, m, 1.0 / d, None, ALU.mult, None, v)
            v = TT(q.V, x, x, bc(m, d), ALU.subtract, v)
            t = AC(tmp, x, ACT.Square, v)
            v = RED(s, tmp, ALU.add, t)
            t = AC(s, s, ACT.Sqrt, v, bias=epsL, scale=1.0 / d)
            v = RCP(s, s, t)
            return TT(q.V, x, x, bc(s, d), ALU.mult, v)

        def post(gi):
            w0 = gi * g4
            gw = min(g4, NW - w0)
            b = gi % 2
            F = gw * P
            for i in range(gw):
                cl = (w0 + i) * P
                MM(psum[:, 2 * b, i * P:(i + 1) * P], acc[:, 0, cl:cl + P], zgw, v_z, *([Hn["z", gi - 2]] if gi > 1 else []))
                t = MM(psum[:, 2 * b + 1, i * P:(i + 1) * P], acc[:, 1, cl:cl + P], zgw)
            Z, T_ = z[:, b, 0:F], zt[:, b, 0:F]
            X = xn[:, b, 0:F]
            dx = slot(f"xn{b}").dma(q.S, lambda e: e.dma_start(
                X.rearrange("p (w f) -> p w f", f=P),
                a["x"][w0 * P:(w0 + gw) * P, :].rearrange("(w p) f -> p w f", p=P)),
                *([Hn["x", gi - 2]] if gi > 1 else []))
            L = lse[:, w0:w0 + gw, :].rearrange("p w h -> p (w h)")
            D = deg[:, w0:w0 + gw, :]
            c_ = hm[:, b, 0:gw * 8]
            v = TT(q.V, heads(T_), heads(psum[:, 2 * b + 1, 0:F]), bc(L, HD), ALU.mult, t)
            v = TT(q.V, Z, psum[:, 2 * b, 0:F], T_, ALU.subtract, v)
            Hn["z", gi] = v
            v = TT(q.V, c_.rearrange("p (w h) -> p w h", h=8), lse[:, w0:w0 + gw, :],
                   D[:, :, 0:1].to_broadcast([P, gw, 8]), ALU.mult, v)
            v = TT(q.V, c_.rearrange("p (w h) -> p w h", h=8), D[:, :, 1:9], c_.rearrange("p (w h) -> p w h", h=8), ALU.subtract, v)
            bz4 = bz.unsqueeze(1).to_broadcast([P, gw, P])
            c4 = c_.rearrange("p (w h) -> p w h", h=8)
            w3 = lambda x: x.rearrange("p (w f) -> p w f", f=P)
            for i in range(gw):
                v = TT(q.V, heads(T_[:, i * P:(i + 1) * P]), heads(bz), bc(c_[:, i * 8:i * 8 + 8], HD), ALU.mult, v, v_bz)
            v = TT(q.V, Z, Z, T_, ALU.add, v)
            v = TT(q.V, w3(Z), w3(Z), mid(zg_in[:, 0, :], gw), ALU.add, v)
            v = TS(q.V, Z, Z, 0.0, None, ALU.max, None, v)
            v = layer_norm_nodes(heads(Z), heads(T_), c_, hs[:, b, 0:gw * 8], gw * 8, HD, gi, v)
            v = TT(q.V, w3(Z), w3(Z), mid(zg_in[:, 1, :], gw), ALU.mult, v)
            v = TT(q.V, w3(Z), w3(Z), mid(zg_in[:, 2, :], gw), ALU.add, v)
            v = TT(q.V, Z, Z, X, ALU.add, v, dx)
            Hn["x", gi] = v
            v = layer_norm_nodes(w3(Z), w3(T_), nm[:, b, 0:gw], hs[:, b, 0:gw], gw, P, gi, v)
            Hn["o", gi] = q.V(lambda e: e.tensor_copy(x1[:, w0:w0 + gw, :], w3(Z)), v)

        NG = -(-NW // g4)
        for gi in range(NG):
            post(gi)
        join()

        top[0] = perm
        wl = mem(3, P)
        bl_ = mem(3, P)
        h = mem(NW, P)
        gt = mem(2, ST, P)
        ohh = mem(2, ST, WN)
        dc2 = mem(ST)
        xT2 = mem(2, P)
        accf = mem(NC)
        assert top[0] <= phase3
        top[0] = x1s
        dis_ = mem(NW)
        cur = mem(NW, P)
        prv = mem(NW, P)
        tz = mem(2, g4 * P)
        ns = mem(2, g4)
        s4 = slot("w3")
        for i in range(3):
            s4.dma(q.S, lambda e, i=i: e.dma_start(wl[:, i, :], a[f"W{i + 1}"]))
            d4 = s4.dma(q.S, lambda e, i=i: e.dma_start(bl_[:, i, :], a[f"b{i + 1}"].partition_broadcast(P)))
        q.V(lambda e: e.tensor_copy(cur, x1))
        vc = q.V(lambda e: e.tensor_copy(prv, x1))
        epn = mem(1)
        q.V(lambda e: e.memset(epn, 0.0))
        join()

        def convolution(layer):
            Hn = {}
            H = {}
            for w in range(NW):
                b = w % 2
                pre = [Hn["c", w - 2]] if w > 1 else []
                t = TR(psum[:, b, 0:P], cur[:, w, :], ident, *pre)
                pre = [Hn["m", w - 2]] if w > 1 else []
                c = AC(xT2[:, b, :], psum[:, b, 0:P], ACT.Copy, t, *pre)
                Hn["c", w] = c
                pre = [Hn["h", w - 2]] if w > 1 else []
                t = MM(psum[:, 2 + b, 0:P], xT2[:, b, :], wl[:, layer, :], c, *pre)
                Hn["m", w] = t
                v = TS(q.V, h[:, w, :], psum[:, 2 + b, 0:P], dis[:, w:w + 1], None, ALU.mult, None, t)
                Hn["h", w] = v
                dh = slot("ho").dma(q.S, lambda e, w=w: e.dma_start(htab[layer][w * P:(w + 1) * P, :], h[:, w, :]), v)
            va0 = q.V(lambda e: e.memset(accf, 0.0))
            join()

            sxl = {n: sem(f"x_{n}{layer}") for n in ("dve", "pe", "in")}
            q.V.raw(lambda e: e.reg_mov(regs["dve"], 0))
            q.V.raw(lambda e: e.reg_mov(regs["in"], 0))
            q.E.raw(lambda e: e.reg_mov(regs["pe"], 0))

            def fetch(s):
                b = s % 2
                q.G.wait(*get2("add", s - 2))
                for t in range(ST):
                    ix = srci[:, s, t:t + 1]
                    H["g", s] = slot(f"g{b}").dma(q.G, lambda e, t=t, ix=ix: e.indirect_dma_start(
                        gt[:, b, t, :], None, htab[layer], bass.IndirectOffsetOnAxis(ap=ix, axis=0)))

            def get2(*k):
                return [H[k]] if k in H else []

            def parts1(s):
                b = s % 2
                return [(psum[:, b, 0:WN], lambda t: gt[:, b, t, :])]

            for s in range(NS + 1):
                if s < NS:
                    b = s % 2
                    fetch(s)
                    v = TT(q.V, ohh[:, b, :, :], bc(dstrel[:, s, :], WN), mid(iota, ST), ALU.is_equal, *get2("ag", s - 2))
                    if s >= 1:
                        pe_more(s - 1, parts1(s - 1), ohh[:, (s - 1) % 2, :, :], sxl)
                    H["ag", s] = pe_aggregate(s, parts1(s), ohh[:, b, :, :], H["g", s], v, *get2("add", s - 2))
                else:
                    pe_more(s - 1, parts1(s - 1), ohh[:, (s - 1) % 2, :, :], sxl)
                if s >= 1:
                    b = (s - 1) % 2
                    H["add", s - 1] = dve_add(s - 1, [(lambda n: accf[:, bass.ds(n, WN)], psum[:, b, 0:WN])],
                                               ohh[:, b, :, :], dc2, sxl, H["ag", s - 1], *get2("add", s - 2))
            join()

            for gi in range(NG):
                w0 = gi * g4
                gw = min(g4, NW - w0)
                b = gi % 2
                F = gw * P
                for i in range(gw):
                    t = TR(psum[:, b, i * P:(i + 1) * P], accf[:, (w0 + i) * P:(w0 + i + 1) * P], ident,
                           *([Hn["t", gi - 2]] if gi > 1 else []))
                Z = tz[:, b, 0:F].rearrange("p (w f) -> p w f", f=P)
                pre = [Hn["o", gi - 2]] if gi > 1 else []
                v = TT(q.V, Z, psum[:, b, 0:F].rearrange("p (w f) -> p w f", f=P), h[:, w0:w0 + gw, :], ALU.add, t, *pre)
                Hn["t", gi] = v
                v = TT(q.V, Z, Z, bc(dis[:, w0:w0 + gw], P), ALU.mult, v)
                v = TT(q.V, Z, Z, mid(bl_[:, layer, :], gw), ALU.add, v, d4)
                c = cur[:, w0:w0 + gw, :]
                pv = prv[:, w0:w0 + gw, :]
                if layer < 2:
                    t = AC(c, Z, ACT.Square, v)
                    v = RED(ns[:, b, 0:gw], c, ALU.add, t)
                    t = AC(ns[:, b, 0:gw], ns[:, b, 0:gw], ACT.Sqrt, v, bias=epn)
                    v = TS(q.V, ns[:, b, 0:gw], ns[:, b, 0:gw], 1e-8, None, ALU.add, None, t)
                    v = RCP(ns[:, b, 0:gw], ns[:, b, 0:gw], v)
                    v = TT(q.V, Z, Z, bc(ns[:, b, 0:gw], P), ALU.mult, v)
                    Hn["o", gi] = TT(q.V, pv, pv, Z, ALU.add, v)
                else:
                    v = TT(q.V, Z, Z, x1[:, w0:w0 + gw, :], ALU.add, v)
                    v = layer_norm_nodes(Z, c, ns[:, b, 0:gw], h[:, w0:w0 + gw, 0], gw, P, gi, v)
                    Hn["o", gi] = q.V(lambda e, Z=Z, c=c: e.tensor_copy(c, Z), v)
            if layer < 2:
                for gi in range(NG):
                    w0 = gi * g4
                    gw = min(g4, NW - w0)
                    AC(cur[:, w0:w0 + gw, :], prv[:, w0:w0 + gw, :], ACT.Gelu, Hn["o", gi])
                join()
            else:
                v = Hn["o", NG - 1]
                nf = N // P
                so = slot("out")
                do_ = so.dma(q.S, lambda e: e.dma_start(out[0:nf * P, :].rearrange("(w p) f -> p w f", p=P), cur[:, 0:nf, :]), v)
                if N % P:
                    do_ = so.dma(q.S, lambda e: e.dma_start(out[nf * P:N, :], cur[0:N % P, nf, :]), v)
                join(False)

        for layer in range(3):
            convolution(layer)

        block = ctx.enter_context(nc.Block())

        @block.sync
        def _(e):
            for f in q.S.ops:
                f(e)

        @block.gpsimd
        def _(e):
            for f in q.G.ops:
                f(e)

        @block.scalar
        def _(e):
            for f in q.A.ops:
                f(e)

        @block.vector
        def _(e):
            for f in q.V.ops:
                f(e)

        @block.tensor
        def _(e):
            for f in q.E.ops:
                f(e)


def layout(inp):
    c = np.ascontiguousarray
    g = {k: np.asarray(v) for k, v in inp.items()}
    N, E = g["x"].shape[0], g["src"].shape[0]
    NW, NS = -(-N // P), -(-E // SE)
    NP, EP = NW * P, NS * SE
    r = {}
    x = np.zeros((NP, P), np.float32)
    x[:N] = g["x"]
    r["x"], r["xT"] = x, c(x.T)
    e = np.zeros((EP, P), np.float32)
    e[:E] = g["edge_attr_128"]
    r["xe"] = c(e.reshape(NS, P, ST, P).transpose(0, 3, 2, 1)).reshape(NS, P, SE)
    src = np.zeros(EP, np.int32)
    src[:E] = g["src"]
    dst = (N + np.minimum(np.maximum(np.arange(EP) - E, 0) * max(NP - N, 1) // max(EP - E, 1), max(NP - N - 1, 0))).astype(np.int32)
    dst[:E] = g["dst"]
    spread = lambda v: c(v.reshape(NS, P, ST).transpose(1, 0, 2)).reshape(P, NS * ST)
    r["src"], r["dst"] = spread(src), spread(dst)
    r["ends"] = c(np.stack([dst.reshape(NS, SE)[:, 0], dst.reshape(NS, SE)[:, -1]]))
    for n in ("Wq", "Wk", "Wv", "Wke", "Wve"):
        r[n] = c(g["L0_gnn_" + n].transpose(1, 0, 2)).reshape(P, P)

    def blocks(w):
        o = np.zeros((P, P), np.float32)
        for h in range(8):
            o[16 * h:16 * h + 16, 16 * h:16 * h + 16] = w
        return o

    tile = lambda v: np.tile(v, 8).reshape(1, P)
    L = lambda n: g["L0_gnn_" + n]
    for n in ("relk", "relv"):
        r[n + "_top"], r[n + "_bot"] = blocks(L(n + "_W")[:16]), blocks(L(n + "_W")[16:])
        r[n + "_b"] = tile(L(n + "_b"))
    r["cols"] = c(np.stack([L(n).reshape(P) for n in ("gke", "gve", "gk", "gv", "bke", "bve", "bk", "bv")], 1))
    r["relv_cols"] = c(np.stack([np.tile(L("relv_g"), 8), np.tile(L("relv_beta"), 8)], 1))
    r["gq"], r["bq"] = L("gq").reshape(P), L("bq").reshape(P)
    r["relk_g"], r["relk_beta"] = np.tile(L("relk_g"), 8), np.tile(L("relk_beta"), 8)
    r["zw"] = blocks(L("z_W"))
    for n in ("z_b", "z_g", "z_beta"):
        r[n] = np.tile(L(n), 8)
    for i in "123":
        r["W" + i], r["b" + i] = g["L1_gnn_W" + i], g["L1_gnn_b" + i]
    r["ident"] = np.eye(P, dtype=np.float32)
    r["iota"] = np.arange(WN, dtype=np.float32)
    return r, NW, NS, N


def kernel(**inputs):
    import concourse.bacc as bacc
    from concourse.bass_utils import run_bass_kernel_spmd

    r, NW, NS, N = layout(inputs)
    nc = bacc.Bacc("TRN2", target_bir_lowering=False, num_devices=1)
    a = {n: nc.dram_tensor("in_" + n, list(v.shape), mybir.dt.from_np(v.dtype), kind="ExternalInput").ap()
         for n, v in r.items()}
    out = nc.dram_tensor("out", [N, P], F32, kind="ExternalOutput").ap()
    gnn(nc, a, out, NW, NS, N)
    res = run_bass_kernel_spmd(nc, [{"in_" + n: v for n, v in r.items()}], core_ids=[0])
    return res.results[0]["out"]
```

```python
import concourse.bass as bass
import numpy as np
from concourse import mybir

F32 = mybir.dt.float32
I32 = mybir.dt.int32
F16 = mybir.dt.float16
BF16 = mybir.dt.bfloat16
ALU = mybir.AluOpType
ACT = mybir.ActivationFunctionType
AX = mybir.AxisListType.X

P = 128
WN = 64
ST = 8
SE = P * ST
NEG = -1.0e30
WD = 40


class Track:

    def __init__(self, sem, lag=None):
        self.sem, self.n, self.ops, self.seen, self.lag = sem, 0, [], {}, lag

    def wait(self, *tokens):
        for sem, val in tokens:
            if self.seen.get(sem.name, 0) < val:
                self.seen[sem.name] = val
                self.ops.append(lambda e, s=sem, v=val: e.wait_ge(s, v))

    def __call__(self, fn, *tokens):
        self.wait(*tokens)
        if self.lag is not None and self.n > self.lag:
            self.wait((self.sem, self.n - self.lag))
        self.n += 1
        self.ops.append(lambda e, s=self.sem: fn(e).then_inc(s, 1))
        return (self.sem, self.n)

    def raw(self, fn, *tokens):
        self.wait(*tokens)
        self.ops.append(fn)

    def now(self):
        return (self.sem, self.n)


class Slot:

    def __init__(self, sem):
        self.sem, self.n = sem, 0

    def dma(self, track, fn, *tokens):
        track.wait(*tokens)
        self.n += 16
        track.ops.append(lambda e: fn(e).then_inc(self.sem, 16))
        return (self.sem, self.n)

    def now(self):
        return (self.sem, self.n)


def gnn(nc, a, out, NW, NS, N):
    from contextlib import ExitStack

    NP = NW * P
    EP = NS * SE
    NC = NP + WN
    NB = EP // 64
    HD = 16

    with ExitStack() as ctx:
        arena = ctx.enter_context(nc.sbuf_tensor("arena", [P, 53100], F32))
        psum = ctx.enter_context(nc.psum_tensor("ps", [P, 8, 512], F32))
        kvp = nc.dram_tensor("kvp", [NP, 256], F32).ap()
        qtab = nc.dram_tensor("qtab", [NP, 136], F32).ap()
        qkd = nc.dram_tensor("qkd", [NB, 512], F32).ap()
        adj = nc.dram_tensor("adj", [P, (NP + P) * NW], BF16).ap()
        htab = [nc.dram_tensor(f"htab{i}", [NP, P], F32).ap() for i in range(3)]

        sem = lambda n: ctx.enter_context(nc.semaphore(n))
        tracks = {}
        slots = {}
        phase = [0]

        def slot(name):
            name = f"{name}_{phase[0]}"
            if name not in slots:
                slots[name] = Slot(sem("d_" + name))
            return slots[name]

        class Q:
            pass

        q = Q()
        q.V, q.A = Track(sem("s_dve"), 1), Track(sem("s_act"), 1)
        q.E, q.G, q.S = [Track(sem(f"s_{n}")) for n in ("pe", "pool", "sp")]
        allq = [q.V, q.A, q.E, q.G, q.S]

        kept = {}

        def join(new=""):
            q.V(lambda e: e.memset(mark[0:1, 8:9], 0.0), q.V.now())
            here = f"_{phase[0]}"
            ends = [t.now() for t in allq if t.n] + [s.now() for n, s in slots.items() if s.n and n.endswith(here)]
            for t in allq:
                t.wait(*ends)
            if new is not None:
                kept[phase[0]] = [(t.sem, t.n) for t in allq]
                phase[0] = new or len(kept)
                if phase[0] not in kept:
                    kept[phase[0]] = [(sem(f"s_{n}{phase[0]}"), 0) for n in ("dve", "act", "pe", "pool", "sp")]
                for t, (t.sem, t.n) in zip(allq, kept[phase[0]]):
                    pass

        def branch(i):
            held = []

            def enter(e):
                n = e.value_load(flags[0:1, i:i + 1], min_val=0, max_val=1)
                held.append(e.If(n > 0))
                held[-1].__enter__()
            for t in allq:
                t.ops.append(enter)

            def close():
                for t in allq:
                    t.ops.append(lambda e: held.pop().__exit__(None, None, None))
            return close

        top = [0]

        def mem(*shape, dt=F32, rows=P):
            n = int(np.prod(shape))
            o = top[0]
            top[0] += n
            assert top[0] <= 53100, top[0]
            ap = arena[0:rows, o:o + n]
            if dt is not F32:
                ap = ap.bitcast(dt)
            if len(shape) == 2:
                ap = ap.rearrange("p (a b) -> p a b", b=shape[1])
            if len(shape) == 3:
                ap = ap.rearrange("p (a b c) -> p a b c", b=shape[1], c=shape[2])
            return ap

        def bc(ap, n):
            return ap.unsqueeze(len(ap.shape)).to_broadcast(list(ap.shape) + [n])

        def mid(ap, n):
            return ap.unsqueeze(1).to_broadcast([ap.shape[0], n] + list(ap.shape[1:]))

        def heads(ap):
            return ap.rearrange("p (h d) -> p h d", d=HD)

        def TT(t, o, x, y, op, *w):
            return t(lambda e: e.tensor_tensor(o, x, y, op), *w)

        def TS(t, o, x, s1, s2, op0, op1, *w):
            if s2 is None:
                return t(lambda e: e.tensor_scalar(o, x, s1, None, op0), *w)
            return t(lambda e: e.tensor_scalar(o, x, s1, s2, op0, op1), *w)

        def RED(o, x, op, *w):
            return q.V(lambda e: e.tensor_reduce(o, x, AX, op), *w)

        def RCP(o, x, *w):
            return q.V(lambda e: e.reciprocal(o, x), *w)

        def AC(o, x, f, *w, bias=None, scale=1.0):
            if bias is None:
                return q.A(lambda e: e.activation(o, x, f, scale=scale), *w)
            return q.A(lambda e: e.activation(o, x, f, bias=bias, scale=scale), *w)

        def MM(o, l, r, *w, start=True, stop=True):
            return q.E(lambda e: e.matmul(o, l, r, start=start, stop=stop), *w)

        def TR(o, x, ident, *w):
            return q.E(lambda e: e.transpose(o, x, ident), *w)

        ident = mem(P)
        iota = mem(WN)
        ones = mem(P)
        epsL = mem(1)
        mark = mem(16)
        marks = [0]
        dstrel = mem(NS, ST)
        srci = mem(NS, ST, dt=I32)
        binfo = mem(NS, 2, dt=I32, rows=1)
        deg = mem(NW, 9)
        nbi = mem(1, dt=I32, rows=1)
        flags = mem(2, dt=I32, rows=1)
        perm = top[0]

        s0 = slot("const")
        c_id = s0.dma(q.S, lambda e: e.dma_start(ident, a["ident"]))
        s0.dma(q.S, lambda e: e.dma_start(iota, a["iota"].partition_broadcast(P)))
        c_all = s0.dma(q.S, lambda e: e.dma_start(srci, a["src"].rearrange("p (s t) -> p s t", t=ST)))
        m_one = q.V(lambda e: e.memset(ones, 1.0))
        m_eps = q.V(lambda e: e.memset(epsL, 1e-5))

        dsti = mem(NS * ST, dt=I32)
        dstf = mem(NS, ST)
        bl = mem(2, NS, dt=I32, rows=1)
        blf = mem(2, NS, rows=1)
        nx = mem(NS, dt=I32, rows=1)
        s1 = slot("dst")
        s1.dma(q.S, lambda e: e.dma_start(dsti, a["dst"]))
        s1.dma(q.S, lambda e: e.dma_start(bl[:, 0:1, :].rearrange("p a s -> p (a s)"), a["ends"][0:1, :]))
        d_in = s1.dma(q.S, lambda e: e.dma_start(bl[:, 1:2, :].rearrange("p a s -> p (a s)"), a["ends"][1:2, :]))
        v = q.V(lambda e: e.tensor_copy(dstf, dsti.rearrange("p (s t) -> p s t", t=ST)), d_in)
        v = q.V(lambda e: e.tensor_copy(blf, bl), d_in)
        v1 = q.V(lambda e: e.tensor_copy(binfo[:, :, 0], bl[:, 0, :]), d_in)
        v2 = TT(q.V, blf[:, 1, :], blf[:, 1, :], blf[:, 0, :], ALU.subtract, v)
        v2 = q.V(lambda e: e.tensor_copy(nx, blf[:, 1, :]), v2)
        v_bi = q.V(lambda e: e.tensor_single_scalar(binfo[:, :, 1], nx, 6, ALU.logical_shift_right), v2)
        e1 = MM(psum[:, 0, 0:NS], ones[0:1, :], blf[:, 0, :], v, m_one)
        v_dr = TT(q.V, dstrel, dstf, bc(psum[:, 0, 0:NS], ST), ALU.subtract, e1)

        w5 = mem(5 * 8, HD)
        wm = mem(5 * 8)
        W5 = w5.rearrange("p a d -> p (a d)")
        Wn = W5[:, 0:384]
        W512 = mem(512)
        bdt = mem(2 * 8, HD)
        bdb = mem(2 * 8, HD)
        bm = mem(32)
        cols = mem(8)
        TK = mem(256)
        BK = mem(256)
        wT = mem(256)
        rb = mem(16, HD, rows=1)
        rbm = mem(16, rows=1)
        crow = mem(256, rows=1)
        G1 = mem(P)
        B1 = mem(P)
        G2 = mem(P)
        rows_in = mem(4, P)
        qbc = mem(8)
        s2 = slot("w")
        for i, n in enumerate(("Wq", "Wk", "Wv", "Wke", "Wve")):
            s2.dma(q.S, lambda e, i=i, n=n: e.dma_start(W5[:, i * P:(i + 1) * P], a[n]))
        for i, n in enumerate(("relk", "relv")):
            s2.dma(q.S, lambda e, i=i, n=n: e.dma_start(bdt.rearrange("p a d -> p (a d)")[:, i * P:(i + 1) * P], a[n + "_top"]))
            s2.dma(q.S, lambda e, i=i, n=n: e.dma_start(bdb.rearrange("p a d -> p (a d)")[:, i * P:(i + 1) * P], a[n + "_bot"]))
            s2.dma(q.S, lambda e, i=i, n=n: e.dma_start(rb.rearrange("p a d -> p (a d)")[:, i * P:(i + 1) * P], a[n + "_b"]))
        s2.dma(q.S, lambda e: e.dma_start(cols, a["cols"]))
        for i, n in enumerate(("gq", "bq", "relk_g", "relk_beta")):
            d_w = s2.dma(q.S, lambda e, i=i, n=n: e.dma_start(rows_in[:, i, :], a[n].partition_broadcast(P)))

        def center(x, m, n, *w):
            v = RED(m, x, ALU.add, *w)
            v = TS(q.V, m, m, 1.0 / HD, None, ALU.mult, None, v)
            return TT(q.V, x, x, bc(m, HD), ALU.subtract, v)

        vw = center(w5, wm, 40, d_w)
        vt = center(bdt, bm[:, 0:16], 16, d_w)
        vb = center(bdb, bm[:, 16:32], 16, d_w)
        vr = center(rb, rbm, 16, d_w)
        BT = bdt.rearrange("p a d -> p (a d)")
        BB = bdb.rearrange("p a d -> p (a d)")
        for i in range(2):
            vk = TS(q.V, TK[:, i * P:(i + 1) * P], BT[:, i * P:(i + 1) * P], cols[:, i:i + 1], None, ALU.mult, None, vt)
            vk = TS(q.V, BK[:, i * P:(i + 1) * P], BB[:, i * P:(i + 1) * P], cols[:, 2 + i:3 + i], None, ALU.mult, None, vb)
        t = TR(psum[:, 1, 0:P], W5[:, 384:512], ident, vw, c_all)
        t = TR(psum[:, 1, P:2 * P], W5[:, 512:640], ident)
        v = q.V(lambda e: e.tensor_copy(wT, psum[:, 1, 0:256]), t)
        v = q.V(lambda e: e.tensor_copy(W512[:, 0:256], W5[:, 384:640]))
        for i in range(2):
            t = MM(psum[:, 2, i * P:(i + 1) * P], wT[:, i * P:(i + 1) * P], TK[:, i * P:(i + 1) * P], v)
        v_w5 = q.V(lambda e: e.tensor_copy(W512[:, 256:512], psum[:, 2, 0:256]), t)
        for i in range(2):
            o = psum[0:1, 3, i * P:(i + 1) * P]
            MM(o, cols[:, 4 + i:5 + i], BT[:, i * P:(i + 1) * P], stop=False)
            MM(o, cols[:, 6 + i:7 + i], BB[:, i * P:(i + 1) * P], start=False, stop=False)
            t = MM(o, ones[0:1, 0:1], rb.rearrange("p a d -> p (a d)")[:, i * P:(i + 1) * P], vr, start=False)
        v_c = q.V(lambda e: e.tensor_copy(crow, psum[0:1, 3, 0:256]), t)
        v = TS(q.V, rows_in[:, 2:4, :], rows_in[:, 2:4, :], 0.25, None, ALU.mult, None, d_w)
        TT(q.V, G1, rows_in[:, 0, :], rows_in[:, 2, :], ALU.mult, v)
        TT(q.V, B1, rows_in[:, 1, :], rows_in[:, 2, :], ALU.mult)
        TT(q.V, G2, rows_in[:, 0, :], rows_in[:, 3, :], ALU.mult)
        v = TT(q.V, rows_in[:, 1, :], rows_in[:, 1, :], rows_in[:, 3, :], ALU.mult, q.V.now())
        v_g = RED(qbc, heads(rows_in[:, 1, :]), ALU.add, v)

        nsq = mem(2, 384)
        nva = mem(2, 24)
        nsd = mem(2, 24)
        nh = mem(2, 384)
        nq = mem(2, 136)
        nqt = mem(2, P)
        nT = mem(2, 256)
        nkv = mem(2, 256)
        xt = mem(NW, P)
        hist = {}
        XC = 7
        d_x = [slot(f"xt{i}").dma(q.S, lambda e, i=i: e.dma_start(
            xt[:, i * XC:min(NW, (i + 1) * XC), :].rearrange("p w f -> p (w f)"), a["xT"][:, i * XC * P:min(NW, (i + 1) * XC) * P]))
            for i in range(-(-NW // XC))]

        def nA(w):
            b = w % 2
            t = MM(psum[:, b, 0:384], xt[:, w, :], Wn, d_x[w // XC], v_w5, *([hist["h", w - 2]] if w > 1 else []))
            hist["mm", w] = t
            s = AC(nsq[:, b, :], psum[:, b, 0:384], ACT.Square, t, *([hist["var", w - 2]] if w > 1 else []))
            r = RED(nva[:, b, :], heads(nsq[:, b, :]), ALU.add, s)
            hist["var", w] = r
            hist["sd", w] = AC(nsd[:, b, :], nva[:, b, :], ACT.Sqrt, r, m_eps, bias=epsL, scale=1.0 / HD)

        def nB(w):
            b = w % 2
            r = RCP(nva[:, b, :], nsd[:, b, :], hist["sd", w])
            pre = [hist["tr", w - 2]] if w > 1 else []
            h = TT(q.V, heads(nh[:, b, :]), heads(psum[:, b, 0:384]), bc(nva[:, b, :], HD), ALU.mult, r, *pre)
            hist["h", w] = h
            TR(psum[:, 2 + b, 0:P], nh[:, b, P:2 * P], ident, h, *([hist["cT", w - 2]] if w > 1 else []))
            t = TR(psum[:, 2 + b, P:256], nh[:, b, 256:384], ident)
            hist["tr", w] = t
            hist["cT", w] = AC(nT[:, b, :], psum[:, 2 + b, 0:256], ACT.Copy, t,
                               *([hist["mm2", w - 2]] if w > 1 else []))
            pre = [slot(f"qo{b}").now()] if w > 1 else []
            m = TT(q.V, nqt[:, b, :], nh[:, b, 0:P], G2, ALU.mult, v_g, h)
            m1 = TT(q.V, nq[:, b, 0:P], nh[:, b, 0:P], G1, ALU.mult, *pre)
            r = RED(nq[:, b, P:136], heads(nqt[:, b, :]), ALU.add, m)
            TT(q.V, nq[:, b, 0:P], nq[:, b, 0:P], B1, ALU.add, m1)
            t = TT(q.V, nq[:, b, P:136], nq[:, b, P:136], qbc, ALU.add, r)
            slot(f"qo{b}").dma(q.S, lambda e: e.dma_start(qtab[w * P:(w + 1) * P, :], nq[:, b, :]), t)

        def nC(w):
            b = w % 2
            for i in range(2):
                o = psum[:, 4 + b, i * P:(i + 1) * P]
                MM(o, nT[:, b, i * P:(i + 1) * P], BK[:, i * P:(i + 1) * P], hist["cT", w],
                   *([hist["kv", w - 2]] if w > 1 else []), stop=False)
                t = MM(o, ones[0:1, :], crow[:, i * P:(i + 1) * P], v_c, start=False)
            hist["mm2", w] = t
            c = AC(nkv[:, b, :], psum[:, 4 + b, 0:256], ACT.Copy, t,
                   *([slot(f"ko{b}").now()] if w > 1 else []))
            hist["kv", w] = c
            slot(f"ko{b}").dma(q.S, lambda e: e.dma_start(kvp[w * P:(w + 1) * P, :], nkv[:, b, :]), c)

        for w in range(NW + 2):
            if w < NW:
                nA(w)
            if 0 < w <= NW:
                nB(w - 1)
            if w > 1:
                nC(w - 2)

        join()

        W512b = W512
        save = top[0]
        top[0] = perm
        W = mem(512)
        v_w = q.V(lambda e: e.tensor_copy(W, W512b))
        acc = mem(2, NC)
        accq = mem(NC, rows=9)
        XB = 3
        xe = mem(XB, SE)
        GB = 3
        kg = mem(GB, ST, 256)
        qg = mem(GB, ST, 136)
        tu = mem(2, ST, 256)
        sq = mem(2, 512)
        va = mem(3, 32)
        sd = mem(3, 32)
        sq2 = mem(ST, 256)
        va2 = mem(ST, HD)
        sd2 = mem(ST, HD)
        pr = mem(ST, P)
        qr = mem(ST, 8)
        qs = mem(2, ST, 8)
        c1 = mem(ST, 8)
        vals = mem(2, ST * 265)
        agS = mem(265, rows=WN)
        oh = mem(2, ST, WN)
        dc = mem(ST)
        q.V.wait(v_w)
        V0 = q.V(lambda e: e.memset(acc, 0.0), v_w)
        V1 = q.V(lambda e: e.memset(accq, 0.0))
        V2 = q.V(lambda e: e.memset(vals, 1.0))
        xcnt = {}

        def val(b):
            return vals[:, b, :].rearrange("p (t f) -> p t f", f=265)

        regs = {}
        sx = {n: sem("x_" + n) for n in ("dve", "pe", "in", "act", "pt")}

        def init_regs(e, name):
            regs[name] = e.alloc_register("xc_" + name)
            e.reg_mov(regs[name], 0)

        q.V.raw(lambda e: init_regs(e, "dve"))
        q.V.raw(lambda e: init_regs(e, "at"))
        q.V.raw(lambda e: init_regs(e, "in"))
        q.E.raw(lambda e: init_regs(e, "pe"), v_bi)
        q.A.raw(lambda e: init_regs(e, "act"), v_bi)

        def pe_aggregate(s, parts, o_h, *w):
            b = s % 2
            for dst, lhs in parts[:-1]:
                for t in range(ST):
                    q.E.raw(lambda e, dst=dst, lhs=lhs, t=t: e.matmul(dst, lhs(t), o_h[:, t, :], start=t == 0, stop=t == ST - 1), *w)
            dst, lhs = parts[-1]
            for t in range(ST - 1):
                q.E.raw(lambda e, t=t: e.matmul(dst, lhs(t), o_h[:, t, :], start=t == 0, stop=False), *w)
            return q.E(lambda e: e.matmul(dst, lhs(ST - 1), o_h[:, ST - 1, :], start=False, stop=True))

        def pe_more(s, parts, o_h, sx):
            def f(e):
                n = e.value_load(binfo[0:1, s, 1:2], min_val=0, max_val=NP // WN)
                with e.If(n > 0), e.Fori(0, n) as i:
                    e.reg_add(regs["pe"], regs["pe"], 1)
                    e.wait_ge(sx["dve"], e.snap(regs["pe"], min_val=1, max_val=1 << 20))
                    last = None
                    for dst, lhs in parts:
                        for t in range(ST):
                            last = e.matmul(dst, lhs(t), o_h[:, t, :], start=t == 0, stop=t == ST - 1)
                    last.then_inc(sx["pe"], 1)
            q.E.raw(f)

        def dve_add(s, adds, o_h, dc, sx, *w):
            q.V.wait(*w)
            q.V.n += len(adds) + 2
            q_sem, done, na = q.V.sem, q.V.n - 1, len(adds)
            marks[0] = (marks[0] + 1) % 8
            m = marks[0]

            def f(e):
                n0 = e.value_load(binfo[0:1, s, 0:1], min_val=0, max_val=NP)
                for tgt, src in adds:
                    o = tgt(n0)
                    e.tensor_tensor(o, o, src, ALU.add).then_inc(q_sem, 1)
                e.tensor_copy(dc, dstrel[:, s, :]).then_inc(q_sem, 1)
                n = e.value_load(binfo[0:1, s, 1:2], min_val=0, max_val=NP // WN)
                e.reg_mov(regs["at"], n0)
                with e.If(n > 0), e.Fori(0, n) as i:
                    e.reg_add(regs["at"], regs["at"], WN)
                    at = e.snap(regs["at"], min_val=0, max_val=NP)
                    k = e.snap(regs["dve"], min_val=0, max_val=1 << 20)
                    ki = e.snap(regs["in"], min_val=0, max_val=1 << 20)
                    e.wait_ge(q_sem, done)
                    e.tensor_scalar(dc, dc, float(-WN), None, ALU.add).then_inc(sx["in"], 1)
                    e.wait_ge(sx["in"], ki + 1)
                    e.tensor_tensor(o_h, bc(dc, WN), mid(iota, ST), ALU.is_equal).then_inc(sx["dve"], 1)
                    e.wait_ge(sx["pe"], k + 1)
                    for tgt, src in adds:
                        o = tgt(at)
                        e.tensor_tensor(o, o, src, ALU.add).then_inc(sx["in"], 1)
                    e.wait_ge(sx["in"], ki + (1 + na))
                    e.reg_add(regs["dve"], regs["dve"], 1)
                    e.reg_add(regs["in"], regs["in"], 1 + na)
                e.memset(mark[0:1, m:m + 1], 0.0).then_inc(q_sem, 1)
            q.V.ops.append(f)
            return (q_sem, done + 1)

        H = {}

        def get(*k):
            return [H[k]] if k in H else []

        GR = ST // 2

        def load(s):
            b = s % XB
            d = slot(f"xe{b}").dma(q.S, lambda e: e.dma_start(xe[:, b, :], a["xe"][s]), *get("mm", s - XB, GR - 1))
            H["x", s] = d

        def gather(s):
            b = s % GB
            q.G.wait(*get("u", s - GB))
            for t in range(ST):
                ix = srci[:, s, t:t + 1]
                H["kg", s] = slot(f"kg{b}").dma(q.G, lambda e, t=t, ix=ix: e.indirect_dma_start(
                    kg[:, b, t, :], None, kvp, bass.IndirectOffsetOnAxis(ap=ix, axis=0)))
            q.G.wait(*get("qb", s - GB))
            for t in range(ST):
                ix = dsts[:, s, t:t + 1]
                H["qg", s] = slot(f"qg{b}").dma(q.G, lambda e, t=t, ix=ix: e.indirect_dma_start(
                    qg[:, b, t, :], None, qtab, bass.IndirectOffsetOnAxis(ap=ix, axis=0)))

        dsts = mem(NS, ST, dt=I32)
        d_ds = slot("dsts").dma(q.S, lambda e: e.dma_start(dsts, a["dst"].rearrange("p (s t) -> p s t", t=ST)))
        q.G.wait(d_ds)

        def grp(s, g):
            k = s * GR + g
            ps = psum[:, 2 * (k % 3):2 * (k % 3) + 2, :]
            for j in range(2):
                t = 2 * g + j
                H["mm", s, g] = MM(ps[:, j, :], xe[:, s % XB, t * P:(t + 1) * P], W, H["x", s], v_w,
                                   *get("tm", k - 3))
            b = k % 2
            H["sq", k] = AC(sq[:, b, :].rearrange("p (j f) -> p j f", j=2), ps[:, :, 0:256], ACT.Square, H["mm", s, g],
                            *get("va", k - 2))

        def grp1(k):
            H["va", k] = RED(va[:, k % 3, :], heads(sq[:, k % 2, :]), ALU.add, H["sq", k], *get("tm", k - 3))

        def grp2(k):
            b = k % 3
            H["sd", k] = AC(sd[:, b, :], va[:, b, :], ACT.Sqrt, H["va", k], *get("tm", k - 3), bias=epsL, scale=1.0 / HD)

        def grp3(k):
            s, g, b = k // GR, k % GR, k % 3
            ps = psum[:, 2 * (k % 3):2 * (k % 3) + 2, 256:512]
            r = RCP(va[:, b, :], sd[:, b, :], H["sd", k])
            o = tu[:, s % 2, 2 * g:2 * g + 2, :].rearrange("p j (h d) -> p j h d", d=HD)
            H["tm", k] = TT(q.V, o, ps.rearrange("p j (h d) -> p j h d", d=HD),
                            bc(va[:, b, :].rearrange("p (j h) -> p j h", j=2), HD), ALU.mult, r,
                            *get("sq2", s - 2))

        def sup1(s):
            b = s % 2
            u = tu[:, b, :, :]
            H["u", s] = TT(q.V, u, u, kg[:, s % GB, :, :], ALU.add, H["kg", s], H["tm", s * GR + GR - 1])
            H["sq2", s] = AC(sq2, u, ACT.Square, H["u", s], *get("va2", s - 1))
            H["pr", s] = TT(q.V, pr, u[:, :, 0:P], qg[:, s % GB, :, 0:P], ALU.mult, H["u", s], H["qg", s])
            H["qb", s] = q.V(lambda e: e.tensor_copy(c1, qg[:, s % GB, :, P:136]))

        def sup2(s):
            H["qr", s] = RED(qr, pr.rearrange("p t (h d) -> p t h d", d=HD), ALU.add, H["pr", s])
            H["va2", s] = RED(va2, sq2.rearrange("p t (h d) -> p t h d", d=HD), ALU.add, H["sq2", s], *get("sd2", s - 1))
            H["sd2", s] = AC(sd2, va2, ACT.Sqrt, H["va2", s], *get("r2", s - 1), bias=epsL, scale=1.0 / HD)

        def sup3(s):
            b = s % 2
            u = tu[:, b, :, :].rearrange("p t (h d) -> p t h d", d=HD)
            r = RCP(va2, sd2, H["sd2", s])
            H["r2", s] = r
            m = TT(q.V, qs[:, b, :, :], qr, va2[:, :, 0:8], ALU.mult, r, H["qr", s], *get("qo", s - 2), *get("q9", s - 2))
            m = TT(q.V, qs[:, b, :, :], qs[:, b, :, :], c1, ALU.add, m, H["qb", s])
            H["qo", s] = slot(f"qo{b}").dma(q.S, lambda e: e.dma_start(
                qkd[s * 16:(s + 1) * 16, :].rearrange("a (p f) -> (a p) f", f=64), qs[:, b, :, :]), m)
            H["q9", s] = AC(val(b)[:, :, 257:265], qs[:, b, :, :], ACT.Copy, m, V2, *get("add", s - 2))
            H["m2", s] = TT(q.V, c1, qs[:, b, :, :], va2[:, :, 8:16], ALU.mult, m)

        def sup4(s):
            b = s % 2
            u = tu[:, b, :, :].rearrange("p t (h d) -> p t h d", d=HD)
            BV = val(b)[:, :, P:256].rearrange("p t (h d) -> p t h d", d=HD)
            AV = val(b)[:, :, 0:P].rearrange("p t (h d) -> p t h d", d=HD)
            TT(q.V, BV, u[:, :, 8:16, :], bc(va2[:, :, 8:16], HD), ALU.mult, *get("ag", s - 2))
            TT(q.V, AV, u[:, :, 8:16, :], bc(c1, HD), ALU.mult, H["m2", s])
            H["oh", s] = TT(q.V, oh[:, b, :, :], bc(dstrel[:, s, :], WN), mid(iota, ST), ALU.is_equal)

        def agg_tile(e, s, t, o_h):
            return e.matmul(psum[0:WN, 6, 0:265], o_h[:, t, :], val(s % 2)[:, t, :], start=t == 0, stop=t == ST - 1)

        def turned(e, k):
            if k < 2:
                return e.transpose(psum[:, 7, k * WN:(k + 1) * WN], agS[:, k * P:(k + 1) * P], ident[0:WN, 0:WN])
            return e.transpose(psum[0:9, 7, 2 * WN:3 * WN], agS[:, 256:265], ident[0:WN, 0:WN])

        def agg(s, tiles):
            for t in tiles:
                H["ag", s] = q.E(lambda e, t=t: agg_tile(e, s, t, oh[:, s % 2, :, :]), H["oh", s], H["q9", s],
                                 *get("ev", s - 1))

        def evac(s):
            H["ev", s] = AC(agS, psum[0:WN, 6, 0:265], ACT.Copy, H["ag", s], *get("tr", s - 1))

        def tail(s):
            for k in range(3):
                H["tr", s] = q.E(lambda e, k=k: turned(e, k), H["ev", s], *get("add", s - 1))

            def pe_extra(e):
                n = e.value_load(binfo[0:1, s, 1:2], min_val=0, max_val=NP // WN)
                with e.If(n > 0), e.Fori(0, n) as i:
                    k = e.snap(regs["pe"], min_val=0, max_val=1 << 20)
                    e.wait_ge(sx["dve"], k + 1)
                    for t in range(ST):
                        last = agg_tile(e, s, t, oh[:, s % 2, :, :])
                    last.then_inc(sx["pe"], 1)
                    e.wait_ge(sx["act"], k + 1)
                    e.reg_add(regs["pe"], regs["pe"], 1)
                    for j in range(3):
                        last = turned(e, j)
                    last.then_inc(sx["pt"], 1)

            def act_extra(e):
                n = e.value_load(binfo[0:1, s, 1:2], min_val=0, max_val=NP // WN)
                with e.If(n > 0), e.Fori(0, n) as i:
                    k = e.snap(regs["act"], min_val=0, max_val=1 << 20)
                    e.wait_ge(sx["pe"], k + 1)
                    e.activation(agS, psum[0:WN, 6, 0:265], ACT.Copy).then_inc(sx["act"], 1)
                    e.reg_add(regs["act"], regs["act"], 1)

            q.E.raw(pe_extra)
            q.A.raw(act_extra, H["tr", s])
            bank = psum[:, 7, :]
            H["add", s] = dve_add(s, [
                (lambda n: acc[:, :, bass.ds(n, WN)], bank[:, 0:2 * WN].rearrange("p (x n) -> p x n", n=WN)),
                (lambda n: accq[:, bass.ds(n, WN)], bank[0:9, 2 * WN:3 * WN]),
            ], oh[:, s % 2, :, :], dc, {**sx, "pe": sx["pt"]}, H["tr", s], *get("add", s - 1), V1)

        for s in range(2):
            load(s)
            gather(s)
        grp(0, 0)
        for s in range(NS + 1):
            for g in range(GR):
                k = s * GR + g
                if s < NS and g == 1 and s + 2 < NS:
                    load(s + 2)
                if k + 1 < NS * GR:
                    grp((k + 1) // GR, (k + 1) % GR)
                if 0 <= k - 1 < NS * GR:
                    grp3(k - 1)
                if s < NS:
                    grp1(k)
                    grp2(k)
                if s >= 1:
                    if g == 1:
                        sup1(s - 1)
                        if s + 1 < NS:
                            gather(s + 1)
                    if g == 2:
                        sup2(s - 1)
                    if g == 3:
                        sup3(s - 1)
                if s >= 2:
                    if g == 0:
                        sup4(s - 2)
                    if g == 1:
                        agg(s - 2, range(0, 4))
                    if g == 2:
                        agg(s - 2, range(4, 8))
                        evac(s - 2)
                    if g == 3:
                        tail(s - 2)
        sup4(NS - 1)
        agg(NS - 1, range(0, 8))
        evac(NS - 1)
        tail(NS - 1)
        join()

        top[0] = perm
        W = mem(512)
        acc = mem(2, NC)
        accq = mem(NC, rows=9)
        lse = mem(NW, 8)
        ends = mem(NW)
        begs = mem(NW)
        phase3 = max(top[0], perm + 6 * P + NW * P + 2 * ST * (P + WN) + ST + 2 * P + NC + WD * NW,
                     perm + 6 * P + NW * P + NW * 3 * P // 2)
        top[0] = phase3
        GW = 7
        ck2 = mem(2, GW, 128 * 8)
        assert 2 * NP <= 2 * GW * 128 * 8
        cs = arena[0:1, phase3:phase3 + NP]
        zer = arena[0:1, phase3 + NP:phase3 + 2 * NP]
        bi = mem(NW, dt=I32)
        bf = mem(NW)
        nbk = mem(NW)
        nbt = mem(P, rows=1)
        nbm = mem(1, rows=1)
        m0 = q.V(lambda e: e.memset(zer, 0.0))
        v = q.V(lambda e: e.tensor_tensor_scan(cs, accq[0:1, 0:NP], zer, 0.0, ALU.add, ALU.add), m0)
        for w in range(NW):
            t1 = MM(psum[:, w // 32, (w % 32) * 9:(w % 32) * 9 + 9], accq[:, w * P:(w + 1) * P], ident[0:9, 0:9])
        for w in range(NW):
            t2 = MM(psum[:, 2, w:w + 1], cs[0:1, w * P:(w + 1) * P], ones[0:1, 0:1], v)
        nw0 = min(NW, 32)
        q.V(lambda e: e.tensor_copy(deg[:, 0:nw0, :], psum[:, 0, 0:nw0 * 9].rearrange("p (w c) -> p w c", c=9)), t1)
        if NW > 32:
            q.V(lambda e: e.tensor_copy(deg[:, 32:NW, :], psum[:, 1, 0:(NW - 32) * 9].rearrange("p (w c) -> p w c", c=9)))
        v = q.V(lambda e: e.tensor_copy(ends, psum[:, 2, 0:NW]), t2)
        v = TT(q.V, begs, ends, deg[:, :, 0], ALU.subtract, v)
        v = q.V(lambda e: e.tensor_copy(bi, begs), v)
        v = q.V(lambda e: e.tensor_single_scalar(bi, bi, 6, ALU.logical_shift_right), v)
        v = q.V(lambda e: e.tensor_copy(bf, bi), v)
        b64 = mem(NW)
        v1 = TS(q.V, b64, bf, 64.0, None, ALU.mult, None, v)
        v = TT(q.V, begs, begs, b64, ALU.subtract, v1)
        v = TT(q.V, ends, ends, b64, ALU.subtract, v)
        v = RED(nbk[:, 0:1], ends, ALU.max, v)
        t = TR(psum[0:1, 3, 0:P], nbk[:, 0:1], ident, v)
        v = q.V(lambda e: e.tensor_reduce(nbm, psum[0:1, 3, 0:P], AX, ALU.max), t)
        v = TS(q.V, nbm, nbm, 63.0 - 128.0, 0.0, ALU.add, ALU.max, v)
        v = q.V(lambda e: e.tensor_copy(nbi, nbm), v)
        v_nb = q.V(lambda e: e.tensor_single_scalar(nbi, nbi, 6, ALU.logical_shift_right), v)
        join()

        mk = mem(GW, 128)
        mk2 = mem(GW, 128)
        bidx2 = mem(2, GW * 2, dt=I32)
        bjf = mem(GW)
        mx = mem(GW, 8)
        mn = mem(GW, 8)
        cr = mem(GW, 8)
        se = mem(GW, 8)
        sj = mem(GW, 8)
        jo = mem(2)
        iot2 = mem(2 * WN)
        ss = mem(NW, 8)
        mm_ = mem(NW, 8)
        q.V(lambda e: e.tensor_copy(iot2[:, 0:WN], iota))
        v_i2 = TS(q.V, iot2[:, WN:], iota, float(WN), None, ALU.add, None)
        s_lv, s_la, s_lg = sem("l_dve"), sem("l_act"), sem("l_pool")
        q.V.raw(lambda e: init_regs(e, "lv"))
        q.V.raw(lambda e: init_regs(e, "li"))
        q.A.raw(lambda e: init_regs(e, "la"))
        q.G.raw(lambda e: init_regs(e, "lg"))

        def masked(T, x, b0, b1, it, n, w0, gw, prev):
            m = mk[:, 0:gw, 0:n]
            m2 = mk2[:, 0:gw, 0:n]
            i_ = it.unsqueeze(1).to_broadcast([P, gw, n])
            v = T(lambda e: e.tensor_tensor(m, i_, bc(b0, n), ALU.is_ge), prev)
            v = T(lambda e: e.tensor_tensor(m2, i_, bc(b1, n), ALU.is_lt), v)
            v = T(lambda e: e.tensor_tensor(m, m, m2, ALU.mult), v)
            v = T(lambda e: e.tensor_scalar(m, m, -NEG, NEG, ALU.mult, ALU.add), v)
            x3 = x
            v = T(lambda e: e.tensor_tensor(x3, x3, bc(m, 8), ALU.add), v)
            return v

        rounds = {n: sem("l_" + n) for n in ("jo", "j2", "jo2")}

        L = {}

        def blocks_in(w0):
            gw, b = min(GW, NW - w0), w0 // GW % 2
            ck, bidx, bfw = ck2[:, b], bidx2[:, b, :], bf[:, w0:w0 + gw]
            v = None
            for j in range(2):
                v = TS(q.V, bjf[:, 0:gw], bfw, float(j), float(NB - 1), ALU.add, ALU.min, v_i2, q.V.now())
                v = q.V(lambda e, j=j: e.tensor_copy(bidx[:, j * GW:j * GW + gw], bjf[:, 0:gw]), v)
            for i in range(gw):
                for j in range(2):
                    L["in", w0] = slot(f"ck{b}").dma(q.G, lambda e, i=i, j=j: e.indirect_dma_start(
                        ck[:, i, j * 512:(j + 1) * 512], None, qkd,
                        bass.IndirectOffsetOnAxis(ap=bidx[:, j * GW + i:j * GW + i + 1], axis=0)), v, *([L["end", w0 - 2 * GW]] if w0 >= 2 * GW else []))

        def log_sum(w0):
            gw, b = min(GW, NW - w0), w0 // GW % 2
            ck, bidx, bfw = ck2[:, b], bidx2[:, b, :], bf[:, w0:w0 + gw]
            b0, b1 = begs[:, w0:w0 + gw], ends[:, w0:w0 + gw]
            dk = L["in", w0]
            X = ck[:, 0:gw, :].rearrange("p w (i h) -> p w i h", h=8)
            v = masked(q.V, X, b0, b1, iot2, 128, w0, gw, dk)
            XH = ck[:, 0:gw, :].rearrange("p w (i h) -> p w h i", h=8)
            m_, s_ = mx[:, 0:gw, :], se[:, 0:gw, :]
            v = RED(m_, XH, ALU.max, v)
            v = TT(q.V, X, X, m_.unsqueeze(2).to_broadcast([P, gw, 128, 8]), ALU.subtract, v)
            t = AC(ck[:, 0:gw, :], ck[:, 0:gw, :], ACT.Exp, v)
            v = RED(s_, XH, ALU.add, t)

            s_ld = sem(f"l_dma{w0}")
            s_jo, s_j2, s_jo2 = rounds["jo"], rounds["j2"], rounds["jo2"]
            sem_v, done = q.V.sem, q.V.n

            def pool_more(e, s_ld=s_ld, gw=gw):
                n = e.value_load(nbi[0:1, 0:1], min_val=0, max_val=NB)
                with e.If(n > 0), e.Fori(0, n) as j:
                    k = e.snap(regs["lg"], min_val=0, max_val=1 << 16)
                    e.wait_ge(s_lg, k + 1)
                    e.reg_add(regs["lg"], regs["lg"], 1)
                    for i in range(gw):
                        e.indirect_dma_start(ck[:, i, 0:512], None, qkd,
                                             bass.IndirectOffsetOnAxis(ap=bidx[:, i:i + 1], axis=0)).then_inc(s_ld, 16)

            def act_more(e, w0=w0, gw=gw):
                n = e.value_load(nbi[0:1, 0:1], min_val=0, max_val=NB)
                with e.If(n > 0), e.Fori(0, n) as j:
                    ki = e.snap(regs["la"], min_val=0, max_val=1 << 20)
                    e.wait_ge(s_lv, ki + (NSTEP - NTAIL))
                    e.reg_add(regs["la"], regs["la"], NSTEP)
                    e.activation(cr[:, 0:gw, :], cr[:, 0:gw, :], ACT.Exp).then_inc(s_la, 1)
                    e.activation(ck[:, 0:gw, 0:512], ck[:, 0:gw, 0:512], ACT.Exp).then_inc(s_la, 1)

            NSTEP, NTAIL = 17, 4

            def dve_more(e, s_ld=s_ld, sem_v=sem_v, done=done, w0=w0, gw=gw, b0=b0, b1=b1, bfw=bfw, m_=m_, s_=s_):
                n = e.value_load(nbi[0:1, 0:1], min_val=0, max_val=NB)
                X = ck[:, 0:gw, 0:512].rearrange("p w (i h) -> p w i h", h=8)
                XH = ck[:, 0:gw, 0:512].rearrange("p w (i h) -> p w h i", h=8)
                n_, c_, j_ = mn[:, 0:gw, :], cr[:, 0:gw, :], sj[:, 0:gw, :]
                step = [0]
                e.wait_ge(sem_v, done)
                e.memset(jo, 2.0).then_inc(s_jo, 1)
                e.wait_ge(s_jo, w0 // GW + 1)
                with e.If(n > 0), e.Fori(0, n) as j:
                    k = e.snap(regs["lv"], min_val=0, max_val=1 << 16)
                    ki = e.snap(regs["li"], min_val=0, max_val=1 << 20)

                    def do(ins):
                        step[0] += 1
                        ins.then_inc(s_lv, 1)
                        e.wait_ge(s_lv, ki + step[0])
                    T = lambda fn, *w: do(fn(e))
                    do(e.tensor_tensor(bjf[:, 0:gw], bfw, jo[:, 0:1].to_broadcast([P, gw]), ALU.add))
                    do(e.tensor_scalar(bidx[:, 0:gw], bjf[:, 0:gw], float(NB - 1), None, ALU.min))
                    e.sem_inc(s_lg, 1)
                    do(e.tensor_scalar(jo[:, 1:2], jo[:, 0:1], 64.0, None, ALU.mult))
                    do(e.tensor_tensor(iot2[:, WN:], iota, jo[:, 1:2].to_broadcast([P, WN]), ALU.add))
                    e.wait_ge(s_ld, (j + 1) * (16 * gw))
                    masked(T, X, b0, b1, iot2[:, WN:], WN, w0, gw, None)
                    do(e.tensor_reduce(n_, XH, AX, ALU.max))
                    do(e.tensor_tensor(n_, n_, m_, ALU.max))
                    do(e.tensor_tensor(c_, m_, n_, ALU.subtract))
                    do(e.tensor_tensor(X, X, n_.unsqueeze(2).to_broadcast([P, gw, WN, 8]), ALU.subtract))
                    assert step[0] == NSTEP - NTAIL, step
                    e.wait_ge(s_la, k * 2 + 2)
                    do(e.tensor_tensor(s_, s_, c_, ALU.mult))
                    do(e.tensor_reduce(j_, XH, AX, ALU.add))
                    do(e.tensor_tensor(s_, s_, j_, ALU.add))
                    e.tensor_copy(m_, n_).then_inc(s_lv, 1)
                    e.wait_ge(s_lv, ki + NSTEP)
                    e.tensor_scalar(jo[:, 0:1], jo[:, 0:1], 1.0, None, ALU.add).then_inc(s_j2, 1)
                    e.wait_ge(s_j2, k + 1)
                    e.reg_add(regs["lv"], regs["lv"], 1)
                    e.reg_add(regs["li"], regs["li"], NSTEP)
                e.tensor_scalar(iot2[:, WN:], iota, float(WN), None, ALU.add).then_inc(s_jo2, 1)
                e.wait_ge(s_jo2, w0 // GW + 1)
            q.G.raw(pool_more)
            q.A.raw(act_more)
            q.V.raw(dve_more)
            q.V(lambda e, w0=w0, gw=gw, s_=s_: e.tensor_copy(ss[:, w0:w0 + gw, :], s_))
            L["end", w0] = q.V(lambda e, w0=w0, gw=gw, m_=m_: e.tensor_copy(mm_[:, w0:w0 + gw, :], m_))

        blocks_in(0)
        for w0 in range(0, NW, GW):
            if w0 + GW < NW:
                blocks_in(w0 + GW)
            log_sum(w0)
            v = L["end", w0]
        t = AC(ss, ss, ACT.Ln, v)
        v = TT(q.V, lse, ss, mm_, ALU.add, t)
        join()

        top[0] = phase3
        x1 = mem(NW, P)
        x1s = top[0]
        dis = mem(NW)
        zg_in = mem(3, P)
        zw = mem(P)
        zgw = mem(P)
        c2 = mem(2)
        bz = mem(P)
        bzr = mem(P, rows=1)
        s3 = slot("z")
        for i, n in enumerate(("z_b", "z_g", "z_beta")):
            s3.dma(q.S, lambda e, i=i, n=n: e.dma_start(zg_in[:, i, :], a[n].partition_broadcast(P)))
        s3.dma(q.S, lambda e: e.dma_start(zw, a["zw"]))
        d3 = s3.dma(q.S, lambda e: e.dma_start(c2, a["relv_cols"]))
        v_z = TS(q.V, zgw, zw, c2[:, 0:1], None, ALU.mult, None, d3)
        t = MM(psum[0:1, 7, 0:P], c2[:, 1:2], zw, d3)
        v = q.V(lambda e: e.tensor_copy(bzr, psum[0:1, 7, 0:P]), t)
        t = MM(psum[:, 7, P:2 * P], ones[0:1, :], bzr, v)
        v_bz = q.V(lambda e: e.tensor_copy(bz, psum[:, 7, P:2 * P]), t)
        v = TS(q.V, dis, deg[:, :, 0], 1.0, None, ALU.add, None)
        t = AC(dis, dis, ACT.Sqrt, v)
        v_dis = RCP(dis, dis, t)
        g4 = 4
        z = mem(2, g4 * P)
        zt = mem(2, g4 * P)
        xn = mem(2, g4 * P)
        hm = mem(2, g4 * 8)
        hs = mem(2, g4 * 8)
        nm = mem(2, g4)
        Hn = {}

        def layer_norm_nodes(x, tmp, m, s, n, d, g, *w):
            v = RED(m, x, ALU.add, *w)
            v = TS(q.V, m, m, 1.0 / d, None, ALU.mult, None, v)
            v = TT(q.V, x, x, bc(m, d), ALU.subtract, v)
            t = AC(tmp, x, ACT.Square, v)
            v = RED(s, tmp, ALU.add, t)
            t = AC(s, s, ACT.Sqrt, v, bias=epsL, scale=1.0 / d)
            v = RCP(s, s, t)
            return TT(q.V, x, x, bc(s, d), ALU.mult, v)

        def post(gi):
            w0 = gi * g4
            gw = min(g4, NW - w0)
            b = gi % 2
            F = gw * P
            for i in range(gw):
                cl = (w0 + i) * P
                MM(psum[:, 2 * b, i * P:(i + 1) * P], acc[:, 0, cl:cl + P], zgw, v_z, *([Hn["z", gi - 2]] if gi > 1 else []))
                t = MM(psum[:, 2 * b + 1, i * P:(i + 1) * P], acc[:, 1, cl:cl + P], zgw)
            Z, T_ = z[:, b, 0:F], zt[:, b, 0:F]
            X = xn[:, b, 0:F]
            dx = slot(f"xn{b}").dma(q.S, lambda e: e.dma_start(
                X.rearrange("p (w f) -> p w f", f=P),
                a["x"][w0 * P:(w0 + gw) * P, :].rearrange("(w p) f -> p w f", p=P)),
                *([Hn["x", gi - 2]] if gi > 1 else []))
            L = lse[:, w0:w0 + gw, :].rearrange("p w h -> p (w h)")
            D = deg[:, w0:w0 + gw, :]
            c_ = hm[:, b, 0:gw * 8]
            v = TT(q.V, heads(T_), heads(psum[:, 2 * b + 1, 0:F]), bc(L, HD), ALU.mult, t)
            v = TT(q.V, Z, psum[:, 2 * b, 0:F], T_, ALU.subtract, v)
            Hn["z", gi] = v
            v = TT(q.V, c_.rearrange("p (w h) -> p w h", h=8), lse[:, w0:w0 + gw, :],
                   D[:, :, 0:1].to_broadcast([P, gw, 8]), ALU.mult, v)
            v = TT(q.V, c_.rearrange("p (w h) -> p w h", h=8), D[:, :, 1:9], c_.rearrange("p (w h) -> p w h", h=8), ALU.subtract, v)
            bz4 = bz.unsqueeze(1).to_broadcast([P, gw, P])
            c4 = c_.rearrange("p (w h) -> p w h", h=8)
            w3 = lambda x: x.rearrange("p (w f) -> p w f", f=P)
            for i in range(gw):
                v = TT(q.V, heads(T_[:, i * P:(i + 1) * P]), heads(bz), bc(c_[:, i * 8:i * 8 + 8], HD), ALU.mult, v, v_bz)
            v = TT(q.V, Z, Z, T_, ALU.add, v)
            v = TT(q.V, w3(Z), w3(Z), mid(zg_in[:, 0, :], gw), ALU.add, v)
            v = TS(q.V, Z, Z, 0.0, None, ALU.max, None, v)
            v = layer_norm_nodes(heads(Z), heads(T_), c_, hs[:, b, 0:gw * 8], gw * 8, HD, gi, v)
            v = TT(q.V, w3(Z), w3(Z), mid(zg_in[:, 1, :], gw), ALU.mult, v)
            v = TT(q.V, w3(Z), w3(Z), mid(zg_in[:, 2, :], gw), ALU.add, v)
            v = TT(q.V, Z, Z, X, ALU.add, v, dx)
            Hn["x", gi] = v
            v = layer_norm_nodes(w3(Z), w3(T_), nm[:, b, 0:gw], hs[:, b, 0:gw], gw, P, gi, v)
            Hn["o", gi] = q.V(lambda e: e.tensor_copy(x1[:, w0:w0 + gw, :], w3(Z)), v)

        NG = -(-NW // g4)
        for gi in range(NG):
            post(gi)
        join()

        top[0] = perm
        wl = mem(3, P)
        bl_ = mem(3, P)
        h = mem(NW, P)
        conv0 = top[0]
        gt = mem(2, ST, P)
        ohh = mem(2, ST, WN)
        dc2 = mem(ST)
        xT2 = mem(2, P)
        accf = mem(NC)
        st16 = mem(WD * NW).bitcast(BF16).rearrange("p (b n) -> p b n", b=2)
        assert top[0] <= phase3
        HW = NW * 3 * P
        hp = arena[:, conv0:conv0 + HW // 2].bitcast(BF16)
        assert conv0 + HW // 2 <= phase3
        top[0] = x1s
        dis_ = mem(NW)
        tz = mem(2, g4 * P)
        ns = mem(2, g4)
        epn = mem(1)
        z1 = mem(1)
        prv = mem(NW, P)
        cur = mem(NW, P)
        cur0 = top[0] - NW * P
        BK_ = 10 * NW
        TW = WD * NW
        ohk = arena[:, cur0:cur0 + 2 * TW].bitcast(BF16).rearrange("p (b n) -> p b n", b=4)
        NT = NS * ST
        top[0] = max(top[0], cur0 + 2 * TW, cur0 - NW * P + 3 * NT + 2 * NS + 1 + max(TW, P) + 8)
        free0 = top[0]
        LO = mem(NT)
        KEY = mem(NT)
        dsi = mem(NS, dt=I32, rows=1)
        ilo = mem(P // 2).bitcast(F16)
        ikey = mem(-(-TW // 2)).bitcast(F16)
        ohl = mem(4 * P // 2).bitcast(BF16).rearrange("p (b n) -> p b n", b=4)
        AW = P * NW
        ablk = arena[:, free0:free0 + AW].bitcast(BF16).rearrange("p (b n) -> p b n", b=2)
        assert free0 + AW <= 53100
        s4 = slot("w3")
        for i in range(3):
            s4.dma(q.S, lambda e, i=i: e.dma_start(wl[:, i, :], a[f"W{i + 1}"]))
            d4 = s4.dma(q.S, lambda e, i=i: e.dma_start(bl_[:, i, :], a[f"b{i + 1}"].partition_broadcast(P)))

        top[0] = cur0 - NW * P
        si = mem(NT, dt=I32)
        di = mem(NT, dt=I32)
        df = mem(NT)
        n0f = mem(NS + 1, rows=1)
        dsf = mem(NS, rows=1)
        i4 = mem(max(TW, P))
        gm = mem(8)
        assert top[0] <= free0
        s5 = slot("adj")
        s5.dma(q.S, lambda e: e.dma_start(si, a["src2"]))
        s5.dma(q.S, lambda e: e.dma_start(di, a["dst2"]))
        d5 = s5.dma(q.S, lambda e: e.dma_start(i4, a["iota2"].partition_broadcast(P)))
        q.V(lambda e: e.tensor_copy(ilo, i4[:, 0:P]), d5)
        q.V(lambda e: e.tensor_copy(ikey[:, 0:TW], i4[:, 0:TW]))
        q.V(lambda e: e.memset(z1, 0.0))
        q.V(lambda e: e.tensor_copy(df, di))
        v = q.V(lambda e: e.tensor_single_scalar(di, si, P - 1, ALU.bitwise_and), q.V.now())
        q.V(lambda e: e.tensor_copy(LO, di), v)
        v = q.V(lambda e: e.tensor_single_scalar(di, si, 7, ALU.logical_shift_right), q.V.now())
        v = q.V(lambda e: e.tensor_copy(KEY, di), v)
        v = q.V(lambda e: e.scalar_tensor_tensor(KEY, df, float(NW), KEY, ALU.mult, ALU.add), v)
        vn = q.V(lambda e: e.memset(n0f[:, NS:NS + 1], float(NP)))
        vn = q.V(lambda e: e.tensor_copy(n0f[:, 0:NS], binfo[:, :, 0]))
        t = MM(psum[:, 0, 0:NS], ones[0:1, :], n0f[:, 0:NS], vn)
        K3 = KEY.rearrange("p (s t) -> p s t", t=ST)
        q.V(lambda e: e.scalar_tensor_tensor(K3, bc(psum[:, 0, 0:NS], ST), -float(NW), K3, ALU.mult, ALU.add), t, v)
        v = TT(q.V, dsf, n0f[:, 1:NS + 1], n0f[:, 0:NS], ALU.subtract, vn)
        v = q.V(lambda e: e.tensor_reduce(gm[0:1, 1:2], dsf, AX, ALU.max), v)
        v = q.V(lambda e: e.tensor_reduce(gm[:, 4:5], deg[:, :, 0], AX, ALU.max))
        t = TR(psum[0:1, 7, 0:P], gm[:, 4:5], ident, v)
        v = q.V(lambda e: e.tensor_reduce(gm[0:1, 2:3], psum[0:1, 7, 0:P], AX, ALU.max), t)
        v = q.V(lambda e: e.tensor_scalar(gm[0:1, 1:2], gm[0:1, 1:2], float(WD), None, ALU.is_ge), v)
        v = q.V(lambda e: e.tensor_scalar(gm[0:1, 2:3], gm[0:1, 2:3], 256.5, None, ALU.is_ge), v)
        v = q.V(lambda e: e.tensor_scalar(gm[0:1, 3:4], n0f[:, 0:1], 0.5, None, ALU.is_ge), v)
        v = q.V(lambda e: e.tensor_reduce(gm[0:1, 6:7], gm[0:1, 1:4], AX, ALU.max), v)
        v = q.V(lambda e: e.tensor_scalar(gm[0:1, 5:6], gm[0:1, 6:7], -1.0, 1.0, ALU.mult, ALU.add), v)
        v = q.V(lambda e: e.tensor_copy(flags, gm[0:1, 5:7]), v)
        TOP = float((WD - 1) * NW)
        v = TS(q.V, dsf, dsf, float(NW), TOP, ALU.mult, ALU.min, v)
        v = q.V(lambda e: e.tensor_copy(dsi, dsf), v)
        join()
        q.V(lambda e: e.tensor_copy(cur, x1))
        vc = q.V(lambda e: e.tensor_copy(prv, x1))
        q.V(lambda e: e.memset(epn, 0.0))
        join("h")

        def convolution(layer):
            Hn = {}
            H = {}
            for w in range(NW):
                b = w % 2
                pre = [Hn["c", w - 2]] if w > 1 else []
                t = TR(psum[:, b, 0:P], cur[:, w, :], ident, *pre)
                pre = [Hn["m", w - 2]] if w > 1 else []
                c = AC(xT2[:, b, :], psum[:, b, 0:P], ACT.Copy, t, *pre)
                Hn["c", w] = c
                pre = [Hn["h", w - 2]] if w > 1 else []
                t = MM(psum[:, 2 + b, 0:P], xT2[:, b, :], wl[:, layer, :], c, *pre)
                Hn["m", w] = t
                v = TS(q.V, h[:, w, :], psum[:, 2 + b, 0:P], dis[:, w:w + 1], None, ALU.mult, None, t)
                Hn["h", w] = v
                dh = slot("ho").dma(q.S, lambda e, w=w: e.dma_start(htab[layer][w * P:(w + 1) * P, :], h[:, w, :]), v)
            q.V(lambda e: e.memset(accf, 0.0))
            join("d")

            def by_edges():
                sxl = {n: sem(f"x_{n}{layer}") for n in ("dve", "pe", "in")}
                q.V.raw(lambda e: e.reg_mov(regs["dve"], 0))
                q.V.raw(lambda e: e.reg_mov(regs["in"], 0))
                q.E.raw(lambda e: e.reg_mov(regs["pe"], 0))

                def fetch(s):
                    b = s % 2
                    q.G.wait(*get2("add", s - 2))
                    for t in range(ST):
                        ix = srci[:, s, t:t + 1]
                        H["g", s] = slot(f"g{b}").dma(q.G, lambda e, t=t, ix=ix: e.indirect_dma_start(
                            gt[:, b, t, :], None, htab[layer], bass.IndirectOffsetOnAxis(ap=ix, axis=0)))

                def get2(*k):
                    return [H[k]] if k in H else []

                def parts1(s):
                    b = s % 2
                    return [(psum[:, b, 0:WN], lambda t: gt[:, b, t, :])]

                for s in range(NS + 1):
                    if s < NS:
                        b = s % 2
                        fetch(s)
                        v = TT(q.V, ohh[:, b, :, :], bc(dstrel[:, s, :], WN), mid(iota, ST), ALU.is_equal, *get2("ag", s - 2))
                        if s >= 1:
                            pe_more(s - 1, parts1(s - 1), ohh[:, (s - 1) % 2, :, :], sxl)
                        H["ag", s] = pe_aggregate(s, parts1(s), ohh[:, b, :, :], H["g", s], v, *get2("add", s - 2))
                    else:
                        pe_more(s - 1, parts1(s - 1), ohh[:, (s - 1) % 2, :, :], sxl)
                    if s >= 1:
                        b = (s - 1) % 2
                        H["add", s - 1] = dve_add(s - 1, [(lambda n: accf[:, bass.ds(n, WN)], psum[:, b, 0:WN])],
                                                   ohh[:, b, :, :], dc2, sxl, H["ag", s - 1], *get2("add", s - 2))
                join("k")

            def adjacency():
                B = {}
                getb = lambda *k: [B[k]] if k in B else []

                def counted(s):
                    for j in range(ST):
                        c = s * ST + j
                        q.V(lambda e, c=c: e.tensor_scalar(ohl[:, c % 4, :], ilo, LO[:, c:c + 1], None, ALU.is_equal),
                            *getb("mm", c - 4))
                        v = q.V(lambda e, c=c: e.tensor_scalar(ohk[:, c % 4, :], ikey[:, 0:TW], KEY[:, c:c + 1], None, ALU.is_equal))
                        for k in range(4):
                            B["mm", c] = q.E(lambda e, c=c, j=j, k=k: e.matmul(
                                psum[:, 4 * (s % 2) + k, 0:BK_], ohl[:, c % 4, :], ohk[:, c % 4, k * BK_:(k + 1) * BK_],
                                start=j == 0, stop=j == ST - 1), v, *getb("cast", s - 2))

                def narrowed(s):
                    B["cast", s] = q.A(lambda e: e.activation(st16[:, s % 2, :].rearrange("p (k n) -> p k n", k=4),
                                                              psum[:, 4 * (s % 2):4 * (s % 2) + 4, 0:BK_], ACT.Copy),
                                       B["mm", s * ST + ST - 1], *getb("out", s - 2), *getb("carry", s - 1))

                def written(s):
                    v = B["cast", s]
                    if s:
                        def carry(e):
                            at = e.value_load(dsi[0:1, s - 1:s], min_val=0, max_val=(WD - 1) * NW)
                            o = st16[:, s % 2, 0:NW]
                            return e.tensor_tensor(o, o, st16[:, (s - 1) % 2, bass.ds(at, NW)], ALU.add)
                        v = B["carry", s] = q.V(carry, v, *getb("carry", s - 1))
                    q.S.wait(*getb("out", s - 1))

                    def put(e):
                        at = e.value_load(binfo[0:1, s, 0:1], min_val=0, max_val=NP)
                        return e.dma_start(adj[:, bass.ds(at * NW, WD * NW)], st16[:, s % 2, :])
                    B["out", s] = slot("adj").dma(q.S, put, v)

                for s in range(NS):
                    counted(s)
                    if s:
                        written(s - 1)
                    narrowed(s)
                written(NS - 1)

            def by_nodes():
                H3 = hp.rearrange("p (w c f) -> p w c f", c=3, f=P)
                v = q.V(lambda e: e.tensor_copy(H3[:, :, 0, :], h))
                v = TT(q.V, cur, h, H3[:, :, 0, :], ALU.subtract, v)
                v = q.V(lambda e: e.tensor_copy(H3[:, :, 1, :], cur), v)
                v = TT(q.V, cur, cur, H3[:, :, 1, :], ALU.subtract, v)
                v_h = q.V(lambda e: e.tensor_copy(H3[:, :, 2, :], cur), v)

                def block(w, done):
                    b = w % 2
                    d = slot(f"ab{b}").dma(q.S, lambda e: e.dma_start(ablk[:, b, :], adj[:, w * P * NW:(w + 1) * P * NW]),
                                           *get3("mm", w - 2))
                    A = ablk[:, b, :].rearrange("p (n c) -> p n c", c=NW)
                    for c in range(NW):
                        t = q.E(lambda e, c=c: e.matmul(psum[:, w % 8, 0:3 * P], A[:, :, c], hp[:, c * 3 * P:(c + 1) * 3 * P],
                                                        start=c == 0, stop=c == NW - 1), d, v_h, *done)
                    N3["mm", w] = t
                    return t

                N3 = {}
                get3 = lambda *k: [N3[k]] if k in N3 else []
                return block

            def after(block):
                for gi in range(NG):
                    w0 = gi * g4
                    gw = min(g4, NW - w0)
                    b = gi % 2
                    F = gw * P
                    Z = tz[:, b, 0:F].rearrange("p (w f) -> p w f", f=P)
                    pre = [Hn["o", gi - 2]] if gi > 1 else []
                    if block:
                        for i in range(gw):
                            t = block(w0 + i, [Hn["t", gi - 2]] if gi > 1 else [])
                            v = RED(Z[:, i, :], psum[:, (w0 + i) % 8, 0:3 * P].rearrange("p (c f) -> p f c", f=P), ALU.add, t, *pre)
                        v = TT(q.V, Z, Z, h[:, w0:w0 + gw, :], ALU.add, v)
                    else:
                        for i in range(gw):
                            t = TR(psum[:, b, i * P:(i + 1) * P], accf[:, (w0 + i) * P:(w0 + i + 1) * P], ident,
                                   *([Hn["t", gi - 2]] if gi > 1 else []))
                        v = TT(q.V, Z, psum[:, b, 0:F].rearrange("p (w f) -> p w f", f=P), h[:, w0:w0 + gw, :], ALU.add, t, *pre)
                    Hn["t", gi] = v
                    v = TT(q.V, Z, Z, bc(dis[:, w0:w0 + gw], P), ALU.mult, v)
                    v = TT(q.V, Z, Z, mid(bl_[:, layer, :], gw), ALU.add, v, d4)
                    c = cur[:, w0:w0 + gw, :]
                    pv = prv[:, w0:w0 + gw, :]
                    if layer < 2:
                        t = AC(c, Z, ACT.Square, v)
                        v = RED(ns[:, b, 0:gw], c, ALU.add, t)
                        t = AC(ns[:, b, 0:gw], ns[:, b, 0:gw], ACT.Sqrt, v, bias=epn)
                        v = TS(q.V, ns[:, b, 0:gw], ns[:, b, 0:gw], 1e-8, None, ALU.add, None, t)
                        v = RCP(ns[:, b, 0:gw], ns[:, b, 0:gw], v)
                        v = TT(q.V, Z, Z, bc(ns[:, b, 0:gw], P), ALU.mult, v)
                        Hn["o", gi] = TT(q.V, pv, pv, Z, ALU.add, v)
                    else:
                        v = TT(q.V, Z, Z, x1[:, w0:w0 + gw, :], ALU.add, v)
                        v = layer_norm_nodes(Z, c, ns[:, b, 0:gw], h[:, w0:w0 + gw, 0], gw, P, gi, v)
                        Hn["o", gi] = q.V(lambda e, Z=Z, c=c: e.tensor_copy(c, Z), v)
                if layer < 2:
                    for gi in range(NG):
                        w0 = gi * g4
                        gw = min(g4, NW - w0)
                        AC(cur[:, w0:w0 + gw, :], prv[:, w0:w0 + gw, :], ACT.Gelu, Hn["o", gi])
                else:
                    v = Hn["o", NG - 1]
                    nf = N // P
                    so = slot("out")
                    do_ = so.dma(q.S, lambda e: e.dma_start(out[0:nf * P, :].rearrange("(w p) f -> p w f", p=P), cur[:, 0:nf, :]), v)
                    if N % P:
                        do_ = so.dma(q.S, lambda e: e.dma_start(out[nf * P:N, :], cur[0:N % P, nf, :]), v)

            close = branch(0)
            if layer == 0:
                adjacency()
                join("d2")
            else:
                join("d2")
            after(by_nodes())
            join("g")
            close()
            close = branch(1)
            by_edges()
            after(None)
            join("h")
            close()

        for layer in range(3):
            convolution(layer)

        block = ctx.enter_context(nc.Block())

        @block.sync
        def _(e):
            for f in q.S.ops:
                f(e)

        @block.gpsimd
        def _(e):
            for f in q.G.ops:
                f(e)

        @block.scalar
        def _(e):
            for f in q.A.ops:
                f(e)

        @block.vector
        def _(e):
            for f in q.V.ops:
                f(e)

        @block.tensor
        def _(e):
            for f in q.E.ops:
                f(e)


def layout(inp):
    c = np.ascontiguousarray
    g = {k: np.asarray(v) for k, v in inp.items()}
    N, E = g["x"].shape[0], g["src"].shape[0]
    NW, NS = -(-N // P), -(-E // SE)
    NP, EP = NW * P, NS * SE
    r = {}
    x = np.zeros((NP, P), np.float32)
    x[:N] = g["x"]
    r["x"], r["xT"] = x, c(x.T)
    e = np.zeros((EP, P), np.float32)
    e[:E] = g["edge_attr_128"]
    r["xe"] = c(e.reshape(NS, P, ST, P).transpose(0, 3, 2, 1)).reshape(NS, P, SE)
    src = np.zeros(EP, np.int32)
    src[:E] = g["src"]
    dst = (N + np.minimum(np.maximum(np.arange(EP) - E, 0) * max(NP - N, 1) // max(EP - E, 1), max(NP - N - 1, 0))).astype(np.int32)
    dst[:E] = g["dst"]
    spread = lambda v: c(v.reshape(NS, P, ST).transpose(1, 0, 2)).reshape(P, NS * ST)
    r["src"], r["dst"] = spread(src), spread(dst)
    r["src2"], r["dst2"] = c(src.reshape(NS * ST, P).T), c(dst.reshape(NS * ST, P).T)
    r["iota2"] = np.arange(max(WD * NW, P), dtype=np.float32)
    r["ends"] = c(np.stack([dst.reshape(NS, SE)[:, 0], dst.reshape(NS, SE)[:, -1]]))
    for n in ("Wq", "Wk", "Wv", "Wke", "Wve"):
        r[n] = c(g["L0_gnn_" + n].transpose(1, 0, 2)).reshape(P, P)

    def blocks(w):
        o = np.zeros((P, P), np.float32)
        for h in range(8):
            o[16 * h:16 * h + 16, 16 * h:16 * h + 16] = w
        return o

    tile = lambda v: np.tile(v, 8).reshape(1, P)
    L = lambda n: g["L0_gnn_" + n]
    for n in ("relk", "relv"):
        r[n + "_top"], r[n + "_bot"] = blocks(L(n + "_W")[:16]), blocks(L(n + "_W")[16:])
        r[n + "_b"] = tile(L(n + "_b"))
    r["cols"] = c(np.stack([L(n).reshape(P) for n in ("gke", "gve", "gk", "gv", "bke", "bve", "bk", "bv")], 1))
    r["relv_cols"] = c(np.stack([np.tile(L("relv_g"), 8), np.tile(L("relv_beta"), 8)], 1))
    r["gq"], r["bq"] = L("gq").reshape(P), L("bq").reshape(P)
    r["relk_g"], r["relk_beta"] = np.tile(L("relk_g"), 8), np.tile(L("relk_beta"), 8)
    r["zw"] = blocks(L("z_W"))
    for n in ("z_b", "z_g", "z_beta"):
        r[n] = np.tile(L(n), 8)
    for i in "123":
        r["W" + i], r["b" + i] = g["L1_gnn_W" + i], g["L1_gnn_b" + i]
    r["ident"] = np.eye(P, dtype=np.float32)
    r["iota"] = np.arange(WN, dtype=np.float32)
    return r, NW, NS, N


def kernel(**inputs):
    import concourse.bacc as bacc
    from concourse.bass_utils import run_bass_kernel_spmd

    r, NW, NS, N = layout(inputs)
    nc = bacc.Bacc("TRN2", target_bir_lowering=False, num_devices=1)
    a = {n: nc.dram_tensor("in_" + n, list(v.shape), mybir.dt.from_np(v.dtype), kind="ExternalInput").ap()
         for n, v in r.items()}
    out = nc.dram_tensor("out", [N, P], F32, kind="ExternalOutput").ap()
    gnn(nc, a, out, NW, NS, N)
    res = run_bass_kernel_spmd(nc, [{"in_" + n: v for n, v in r.items()}], core_ids=[0])
    return res.results[0]["out"]
```
